# Optimizing a Trainium2 kernel written in Bass

```python
import numpy as np
import jax
import jax.numpy as jnp

def _softmax(x, axis=-1):
    return jax.nn.softmax(x, axis=axis)

def _gelu(x):
    return jax.nn.gelu(x, approximate=True)

def _silu(x):
    return jax.nn.silu(x)

def _sigmoid(x):
    return jax.nn.sigmoid(x)

def _layernorm(x, axis=-1, eps=1e-05):
    m = jnp.mean(x, axis=axis, keepdims=True)
    v = jnp.var(x, axis=axis, keepdims=True)
    return (x - m) / jnp.sqrt(v + eps)

def _scatter_add(tgt, idx, src, axis=0):
    return tgt.at[idx].add(src)

def _segment_sum(src, seg, n):
    return jax.ops.segment_sum(src, seg, n)
kernel_name = 'mk_sandwich_d1_jaxref_r2_04111c'

def setup_inputs(seed: int=0):
    np.random.seed(seed)
    _w = jnp.asarray

    def _L0_attn_setup():
        import jax, jax.numpy as jnp
        import numpy as np
        B, S, D_IN = (4, 2048, 512)
        D_HID = 1024
        D_INNER = D_HID // 2
        NB = 8
        LOG_A_SCALE = -8.0
        R_MIN, R_MAX = (0.9, 0.999)

        def _bdl(x, w, b):
            Bb, Ss, d = x.shape
            nb, bin_, bout = w.shape
            xb = x.reshape(Bb, Ss, nb, bin_)
            y = jnp.einsum('bsni,nio->bsno', xb, w) + b.reshape(nb, bout)
            return y.reshape(Bb, Ss, nb * bout)

        def _reference_tuple_inner(x, w_in, b_in, w_gx, b_gx, w_ga, b_ga, a_real_param, a_imag_param, w_out, b_out):
            xh = x @ w_in + b_in
            gate_x = jax.nn.sigmoid(_bdl(xh, w_gx, b_gx))
            gate_a = jax.nn.sigmoid(_bdl(xh, w_ga, b_ga))
            log_a = LOG_A_SCALE * gate_a * jax.nn.softplus(a_real_param)
            log_a_imag = a_imag_param * gate_a
            a = jnp.exp(jax.lax.complex(log_a, log_a_imag))
            xc = jax.lax.complex(xh[..., :D_INNER], xh[..., D_INNER:])
            xc = gate_x * xc
            norm = jnp.sqrt(jnp.maximum(1.0 - jnp.exp(2.0 * log_a), 1e-06))
            xc = norm * xc

            def combine(l, r):
                return (r[0] * l[0], r[0] * l[1] + r[1])
            _, h = jax.lax.associative_scan(combine, (a, xc), axis=1)
            h_m = jnp.concatenate([h.real, h.imag], axis=-1)
            y = h_m @ w_out + b_out
            h_last = h_m[:, -1]
            return (y, h_last)
        key = jax.random.key(seed)
        ks = jax.random.split(key, 10)
        x = jax.random.normal(ks[0], (B, S, D_IN), dtype=jnp.float32)
        w_in = jax.random.normal(ks[1], (D_IN, D_HID), dtype=jnp.float32) / np.sqrt(D_IN)
        b_in = jnp.zeros((D_HID,), jnp.float32)
        bin_, bout = (D_HID // NB, D_INNER // NB)
        w_gx = jax.random.normal(ks[2], (NB, bin_, bout), dtype=jnp.float32) / np.sqrt(bin_)
        b_gx = jnp.zeros((D_INNER,), jnp.float32)
        w_ga = jax.random.normal(ks[3], (NB, bin_, bout), dtype=jnp.float32) / np.sqrt(bin_)
        b_ga = jnp.zeros((D_INNER,), jnp.float32)
        u = jax.random.uniform(ks[4], (D_INNER,))
        a_real = 0.5 * jnp.log(u * (R_MAX ** 2 - R_MIN ** 2) + R_MIN ** 2 + 1e-08)
        a_real_param = jnp.log(jnp.exp(-a_real) - 1.0)
        a_imag_param = jnp.pi * 0.1 * jax.random.uniform(ks[5], (D_INNER,))
        w_out = jax.random.normal(ks[6], (D_HID, D_IN), dtype=jnp.float32) / np.sqrt(D_HID)
        b_out = jnp.zeros((D_IN,), jnp.float32)
        return dict(x=x, w_in=w_in, b_in=b_in, w_gx=w_gx, b_gx=b_gx, w_ga=w_ga, b_ga=b_ga, a_real_param=a_real_param, a_imag_param=a_imag_param, w_out=w_out, b_out=b_out)
    _L0_attn_in = _L0_attn_setup()

    def _L0_ffn_setup():
        import jax, jax.numpy as jnp
        import numpy as np
        E = 8
        TOPK = 2
        PRIME = 11
        HASH_OFF = 7919
        N_SHARED = 1
        key = jax.random.key(seed)
        ks = jax.random.split(key, 8)
        B, T, C, Hs, Hr = (4, 4096, 512, 1024, 512)
        sc = lambda k, shape, fan: jax.random.normal(k, shape, jnp.float32) * fan ** (-0.5)
        return {'x': jax.random.normal(ks[0], (B, T, C), jnp.float32), 't_emb': jax.random.normal(ks[1], (B, C), jnp.float32), 'sw1': sc(ks[2], (C, Hs), C), 'sb1': jnp.zeros((Hs,), jnp.float32), 'sw3': sc(ks[3], (C, Hs), C), 'sb3': jnp.zeros((Hs,), jnp.float32), 'sw2': sc(ks[4], (Hs, C), Hs), 'sb2': jnp.zeros((C,), jnp.float32), 'w1': sc(ks[5], (E, C, Hr), C), 'b1': jnp.zeros((E, Hr), jnp.float32), 'w2': sc(ks[6], (E, Hr, C), Hr), 'b2': jnp.zeros((E, C), jnp.float32)}
    _L0_ffn_in = _L0_ffn_setup()
    _d = {'L0_attn_x': _L0_attn_in['x'], 'L0_attn_w_in': _L0_attn_in['w_in'], 'L0_attn_b_in': _L0_attn_in['b_in'], 'L0_attn_w_gx': _L0_attn_in['w_gx'], 'L0_attn_b_gx': _L0_attn_in['b_gx'], 'L0_attn_w_ga': _L0_attn_in['w_ga'], 'L0_attn_b_ga': _L0_attn_in['b_ga'], 'L0_attn_a_real_param': _L0_attn_in['a_real_param'], 'L0_attn_a_imag_param': _L0_attn_in['a_imag_param'], 'L0_attn_w_out': _L0_attn_in['w_out'], 'L0_attn_b_out': _L0_attn_in['b_out'], 'L0_ffn_t_emb': _L0_ffn_in['t_emb'], 'L0_ffn_sw1': _L0_ffn_in['sw1'], 'L0_ffn_sb1': _L0_ffn_in['sb1'], 'L0_ffn_sw3': _L0_ffn_in['sw3'], 'L0_ffn_sb3': _L0_ffn_in['sb3'], 'L0_ffn_sw2': _L0_ffn_in['sw2'], 'L0_ffn_sb2': _L0_ffn_in['sb2'], 'L0_ffn_w1': _L0_ffn_in['w1'], 'L0_ffn_b1': _L0_ffn_in['b1'], 'L0_ffn_w2': _L0_ffn_in['w2'], 'L0_ffn_b2': _L0_ffn_in['b2']}
    _x0 = _d['L0_attn_x']
    _d['L0_attn_x'] = jax.random.normal(jax.random.fold_in(jax.random.key(seed), 1), (4, 2048, 512), dtype=_x0.dtype)
    del _x0
    return _d

def reference(L0_attn_x, L0_attn_w_in, L0_attn_b_in, L0_attn_w_gx, L0_attn_b_gx, L0_attn_w_ga, L0_attn_b_ga, L0_attn_a_real_param, L0_attn_a_imag_param, L0_attn_w_out, L0_attn_b_out, L0_ffn_t_emb, L0_ffn_sw1, L0_ffn_sb1, L0_ffn_sw3, L0_ffn_sb3, L0_ffn_sw2, L0_ffn_sb2, L0_ffn_w1, L0_ffn_b1, L0_ffn_w2, L0_ffn_b2):

    def _L0_attn_ref(x, w_in, b_in, w_gx, b_gx, w_ga, b_ga, a_real_param, a_imag_param, w_out, b_out):
        import jax, jax.numpy as jnp
        import numpy as np
        B, S, D_IN = (4, 2048, 512)
        D_HID = 1024
        D_INNER = D_HID // 2
        NB = 8
        LOG_A_SCALE = -8.0
        R_MIN, R_MAX = (0.9, 0.999)

        def _bdl(x, w, b):
            Bb, Ss, d = x.shape
            nb, bin_, bout = w.shape
            xb = x.reshape(Bb, Ss, nb, bin_)
            y = jnp.einsum('bsni,nio->bsno', xb, w) + b.reshape(nb, bout)
            return y.reshape(Bb, Ss, nb * bout)

        def _reference_tuple_inner(x, w_in, b_in, w_gx, b_gx, w_ga, b_ga, a_real_param, a_imag_param, w_out, b_out):
            xh = x @ w_in + b_in
            gate_x = jax.nn.sigmoid(_bdl(xh, w_gx, b_gx))
            gate_a = jax.nn.sigmoid(_bdl(xh, w_ga, b_ga))
            log_a = LOG_A_SCALE * gate_a * jax.nn.softplus(a_real_param)
            log_a_imag = a_imag_param * gate_a
            a = jnp.exp(jax.lax.complex(log_a, log_a_imag))
            xc = jax.lax.complex(xh[..., :D_INNER], xh[..., D_INNER:])
            xc = gate_x * xc
            norm = jnp.sqrt(jnp.maximum(1.0 - jnp.exp(2.0 * log_a), 1e-06))
            xc = norm * xc

            def combine(l, r):
                return (r[0] * l[0], r[0] * l[1] + r[1])
            _, h = jax.lax.associative_scan(combine, (a, xc), axis=1)
            h_m = jnp.concatenate([h.real, h.imag], axis=-1)
            y = h_m @ w_out + b_out
            h_last = h_m[:, -1]
            return (y, h_last)
        return _reference_tuple_inner(x, w_in, b_in, w_gx, b_gx, w_ga, b_ga, a_real_param, a_imag_param, w_out, b_out)[0]

    def _L0_ffn_ref(x, t_emb, sw1, sb1, sw3, sb3, sw2, sb2, w1, b1, w2, b2):
        import jax, jax.numpy as jnp
        import numpy as np
        E = 8
        TOPK = 2
        PRIME = 11
        HASH_OFF = 7919
        N_SHARED = 1
        B, T, C = x.shape
        N = B * T
        xf = x.reshape(N, C)
        shared = jax.nn.silu(xf @ sw1 + sb1) * (xf @ sw3 + sb3) @ sw2 + sb2
        tok = jnp.arange(N)
        out = jnp.zeros((N, C), x.dtype)
        for k in range(TOPK):
            exp_ids = (tok * PRIME + k * HASH_OFF) % E
            sort_idx = jnp.argsort(exp_ids)
            xs = xf[sort_idx].reshape(E, N // E, C)
            h = jax.nn.gelu(jnp.einsum('enc,ech->enh', xs, w1) + b1[:, None, :], approximate=False)
            y = jnp.einsum('enh,ehc->enc', h, w2) + b2[:, None, :]
            out = out.at[sort_idx].add(y.reshape(N, C))
        out = out / TOPK
        return ((shared + out) / (N_SHARED + 1)).reshape(B, T, C)
    x = L0_attn_x
    x = x + _layernorm(_L0_attn_ref(_layernorm(x, axis=-1), L0_attn_w_in, L0_attn_b_in, L0_attn_w_gx, L0_attn_b_gx, L0_attn_w_ga, L0_attn_b_ga, L0_attn_a_real_param, L0_attn_a_imag_param, L0_attn_w_out, L0_attn_b_out), axis=-1)
    x = x + _layernorm(_L0_ffn_ref(_layernorm(x, axis=-1), L0_ffn_t_emb, L0_ffn_sw1, L0_ffn_sb1, L0_ffn_sw3, L0_ffn_sb3, L0_ffn_sw2, L0_ffn_sb2, L0_ffn_w1, L0_ffn_b1, L0_ffn_w2, L0_ffn_b2), axis=-1)
    return x

_drawn_inputs = setup_inputs


def setup_inputs(seed=0):
    import zlib

    import numpy as np

    out = dict(_drawn_inputs(seed))
    spreads = {'L0_attn_b_in': (0.0, 0.1),
     'L0_attn_b_gx': (0.0, 0.271),
     'L0_attn_b_ga': (0.0, 0.1),
     'L0_attn_b_out': (0.0, 0.1),
     'L0_ffn_sb1': (0.0, 0.1),
     'L0_ffn_sb3': (0.0, 0.1),
     'L0_ffn_sb2': (0.0, 0.1),
     'L0_ffn_b1': (0.0, 0.1),
     'L0_ffn_b2': (0.0, 0.1)}
    factors = {}
    for name, (base, spread) in spreads.items():
        noise = np.random.default_rng([zlib.crc32(name.encode()), seed]).standard_normal(out[name].shape)
        drawn = base * np.exp(spread * noise) if base else spread * noise
        out[name] = jnp.asarray(drawn.astype(out[name].dtype))
    for name, factor in factors.items():
        out[name] = (out[name] * factor).astype(out[name].dtype)
    return out
```

```python
from contextlib import ExitStack
import math

import concourse.bass as bass
from concourse import mybir

F32 = mybir.dt.float32
F32R = mybir.dt.float32r
ALU = mybir.AluOpType
ACT = mybir.ActivationFunctionType

P = 128
B, S, D = 4, 2048, 512
N = B * S
DH = 1024
KC = D // P
HC = DH // P
T = 512
G = T // P
NT = N // T
TPB = S // T
NE = 8
EPS = 1e-5
MAGIC = 1.5 * 2 ** 23
TWO_PI = 2 * math.pi
LOG_A_SCALE = -8.0
TWO_PI_SAFE = 6.283185
HS = 1024
HR = 512
RING = 4


def wait(eng, sem, n):
    if isinstance(n, int) and n <= 0:
        return
    eng.wait_ge(sem, n)


def after_wait(eng):
    eng.nop(nofuse=True)


def phase_a(nc, d, NT=NT):
    with ExitStack() as ctx:
        def sb(name, shape, dt=F32):
            return ctx.enter_context(nc.sbuf_tensor(name, shape, dt))

        def sem(name):
            return ctx.enter_context(nc.semaphore(name))

        win_hi = sb("win_hi", [P, KC, DH], F32R)
        win_lo = sb("win_lo", [P, KC, DH], F32R)
        wgate = sb("wgate", [P, HC, P])
        wout = sb("wout", [P, HC, D])
        x_in = sb("x_in", [P, G, D])
        x_res = sb("x_res", [P, G, D])
        xn = sb("xn", [P, G, D])
        xt_hi = sb("xt_hi", [P, KC, T], F32R)
        xt_lo = sb("xt_lo", [P, KC, T], F32R)
        xh = sb("xh", [P, 2, KC, T])
        tanh_x = sb("tanh_x", [P, KC, T])
        tanh_a = sb("tanh_a", [P, KC, T])
        mag = sb("mag", [P, KC, T])
        gain = sb("gain", [P, KC, T])
        turns = sb("turns", [P, KC, T])
        frac = sb("frac", [P, KC, T])
        sin = sb("sin", [P, KC, T])
        cos = sb("cos", [P, KC, T])
        h = sb("h", [P, 2, KC, T])
        cross = sb("cross", [P, 2, KC, T])
        ones = sb("ones", [P, T])
        ident = sb("ident", [P, P])
        bout_row = sb("bout_row", [1, D])
        bout_hi = sb("bout_hi", [1, D], F32R)
        bout_lo = sb("bout_lo", [1, D], F32R)
        ones_row = sb("ones_row", [1, P], F32R)
        b_in = sb("b_in", [P, HC])
        b_gate = sb("b_gate", [P, HC])
        a_real = sb("a_real", [P, KC])
        a_imag = sb("a_imag", [P, KC])
        half_turn = sb("half_turn", [P, KC])
        sp = sb("sp", [P, 6, KC])
        mag_k = sb("mag_k", [P, KC])
        mag2_k = sb("mag2_k", [P, KC])
        halfpi = sb("halfpi", [P, 1])
        ln_half = sb("ln_half", [P, 1])
        keep = sb("keep", [P, NT + 1])
        carry = sb("carry", [P, 2, KC])
        neg_half = sb("neg_half", [P, G])
        x_bn = sb("x_bn", [P, G, 6])
        x_mv = sb("x_mv", [P, G, 2])
        x_sc = sb("x_sc", [P, 2, G])
        y_bn = sb("y_bn", [P, G, 6])
        y_mv = sb("y_mv", [P, G, 2])
        y_sc = sb("y_sc", [P, 2, G])
        psum = ctx.enter_context(nc.psum_tensor("psum_a", [P, 8, 512], F32))
        OUT0 = 4

        consts_loaded = sem("consts_loaded")
        win_loaded = sem("win_loaded")
        wout_loaded = sem("wout_loaded")
        win_hi_done = sem("win_hi_done")
        win_lo_done = sem("win_lo_done")
        pool_consts = sem("pool_consts")
        dve_consts = sem("dve_consts")
        dve_small = sem("dve_small")
        act_small = sem("act_small")
        xin_loaded = sem("xin_loaded")
        xres_loaded = sem("xres_loaded")
        x1_stored = sem("x1_stored")
        x_stats = sem("x_stats")
        x_bn_done = sem("x_bn_done")
        xn_done = sem("xn_done")
        x_small = sem("x_small")
        y_small = sem("y_small")
        transposed = sem("transposed")
        xt_hi_done = sem("xt_hi_done")
        xt_lo_done = sem("xt_lo_done")
        win_done = sem("win_done")
        xh_done = sem("xh_done")
        gate_mm_done = sem("gate_mm_done")
        tanh_done = sem("tanh_done")
        inc_done = sem("inc_done")
        turns_done = sem("turns_done")
        round_done = sem("round_done")
        frac_done = sem("frac_done")
        mag_done = sem("mag_done")
        mag2_done = sem("mag2_done")
        z_done = sem("z_done")
        log_done = sem("log_done")
        norm_done = sem("norm_done")
        gain_done = sem("gain_done")
        sin_done = sem("sin_done")
        abs_done = sem("abs_done")
        cos_done = sem("cos_done")
        gsin_done = sem("gsin_done")
        fwd_mul_done = sem("fwd_mul_done")
        fwd_done = sem("fwd_done")
        scan_done = sem("scan_done")
        back_mul_done = sem("back_mul_done")
        h_done = sem("h_done")
        carry_done = sem("carry_done")
        out_done = sem("out_done")
        y_bn_done = sem("y_bn_done")
        y_stats = sem("y_stats")
        y_scaled = sem("y_scaled")
        y_normed = sem("y_normed")
        x1_ready = sem("x1_ready")

        x_rows = d["x"].rearrange("(t g p) d -> t p g d", g=G, p=P)
        x1_rows = d["x1"].rearrange("(t g p) d -> t p g d", g=G, p=P)
        LAST = NT - 1

        def tile_of(rows, t):
            if isinstance(t, int):
                return rows[t]
            return rows[bass.ds(t, 1)].rearrange("o p g d -> p (o g) d")

        def steps(eng, step):
            step(0)
            with eng.Fori(0, (NT - 2) // 2) as i:
                for u in range(2):
                    step(2 * i + (1 + u))
            step(LAST)

        def first(t):
            return isinstance(t, int) and t == 0

        def last(t):
            return isinstance(t, int) and t == LAST

        block = ctx.enter_context(nc.Block())

        @block.sync
        def _(sp_):
            sp_.dma_start(x_in[:], tile_of(x_rows, 0)).then_inc(xin_loaded, 16)
            sp_.dma_start(h[:].rearrange("p a c t -> p (a c t)"),
                          d["w_in"].rearrange("p k n -> p (k n)")).then_inc(win_loaded, 16)
            for dst, src in ((b_in, "b_in"), (b_gate, "b_gate"), (a_real, "a_real"), (a_imag, "a_imag"),
                             (ident, "ident"), (bout_row, "b_out")):
                sp_.dma_start(dst[:], d[src]).then_inc(consts_loaded, 16)
            sp_.dma_start(wgate[:], d["w_gate"]).then_inc(consts_loaded, 16)
            sp_.dma_start(wout[:], d["w_out"]).then_inc(wout_loaded, 16)
            sp_.dma_start(x_res[:], tile_of(x_rows, 0)).then_inc(xres_loaded, 16)
            sp_.wait_ge(xn_done, G)
            sp_.dma_start(x_in[:], tile_of(x_rows, 1)).then_inc(xin_loaded, 16)

            def step(t):
                if not first(t):
                    sp_.wait_ge(x1_ready, G * t)
                    after_wait(sp_)
                    sp_.dma_start(tile_of(x1_rows, t - 1), x_res[:]).then_inc(x1_stored, 16)
                    sp_.wait_ge(x1_stored, 16 * t)
                    after_wait(sp_)
                    sp_.dma_start(x_res[:], tile_of(x_rows, t)).then_inc(xres_loaded, 16)

            def step_in(t):
                sp_.wait_ge(xn_done, G * (t + 2))
                after_wait(sp_)
                sp_.dma_start(x_in[:], tile_of(x_rows, t + 2)).then_inc(xin_loaded, 16)

            step_in(0)
            with sp_.Fori(0, (NT - 2) // 2 - 1) as i:
                for u in range(2):
                    step(2 * i + (1 + u))
                    step_in(2 * i + (1 + u))
            step(NT - 3)
            step_in(NT - 3)
            step(NT - 2)
            step(LAST)
            sp_.wait_ge(x1_ready, G * NT)
            sp_.dma_start(tile_of(x1_rows, LAST), x_res[:]).then_inc(x1_stored, 16)
            sp_.wait_ge(x1_stored, 16 * NT)

        @block.gpsimd
        def _(pool):
            pool.memset(neg_half[:], -0.5).then_inc(pool_consts, 1)
            pool.wait_ge(pool_consts, 1)

            def scales(mv, sc, small, n, done):
                after_wait(pool)
                pool.tensor_scalar(sc[:, 0], mv[:, :, 1], EPS, 1.0, ALU.add, ALU.mult).then_inc(small, 1)
                pool.tensor_scalar(sc[:, 1], mv[:, :, 0], -1.0, 0.0, ALU.mult, ALU.add).then_inc(small, 1)
                pool.wait_ge(small, n + 2)
                w = sc.shape[-1]
                pool.tensor_tensor(sc[:, 0], sc[:, 0], neg_half[:, 0:w], ALU.pow).then_inc(small, 1)
                pool.wait_ge(small, n + 3)
                pool.tensor_tensor(sc[:, 1], sc[:, 1], sc[:, 0], ALU.mult).then_inc(done, 1)

            def norm_x(t):
                pool.wait_ge(x_stats, G * (t + 1))
                wait(pool, xn_done, G * t)
                scales(x_mv[:], x_sc[:], x_small, 4 * t, x_small)
                pool.wait_ge(x_small, 4 * t + 4)
                wait(pool, transposed, G * t)
                after_wait(pool)
                for j in range(G):
                    pool.tensor_scalar(xn[:, j], x_in[:, j], x_sc[:, 0, j:j + 1], x_sc[:, 1, j:j + 1],
                                       ALU.mult, ALU.add).then_inc(xn_done, 1)

            def norm_y(t):
                for j in range(G):
                    pool.wait_ge(y_stats, G * t + j + 1)
                    scales(y_mv[:, j:j + 1], y_sc[:, :, j:j + 1], y_small, 3 * (G * t + j), y_scaled)

            norm_x(0)
            norm_x(1)

            def step(t):
                if not first(t):
                    norm_y(t - 1)
                if not (isinstance(t, int) and t >= NT - 2):
                    norm_x(t + 2)

            step(0)
            with pool.Fori(0, (NT - 2) // 2 - 1) as i:
                for u in range(2):
                    step(2 * i + (1 + u))
            step(NT - 3)
            step(NT - 2)
            step(LAST)
            norm_y(LAST)

        @block.tensor
        def _(pe):
            def transposes(t):
                for j in range(G):
                    pe.wait_ge(xn_done, G * t + j + 1)
                    if j < 2:
                        wait(pe, tanh_done, 2 * HC * t - 4 + 2 * j if not first(t) else 0)
                    else:
                        pe.wait_ge(xt_lo_done, G * t + j - 1)
                    for c in range(KC):
                        mm = pe.transpose(psum[:, j % 2, c * P:(c + 1) * P], xn[:, j, c * P:(c + 1) * P], ident[:])
                    mm.then_inc(transposed, 1)

            def project(t):
                for k, n in enumerate((0, 4, 1, 5, 2, 6, 3, 7)):
                    if k == 0:
                        pe.wait_ge(xt_lo_done, G * (t + 1))
                        wait(pe, tanh_done, 2 * HC * t)
                    if k >= 4:
                        pe.wait_ge(xh_done, HC * t + k - 3)
                    for kc in range(KC):
                        w_hi = win_hi[:, kc, n * P:(n + 1) * P]
                        w_lo = win_lo[:, kc, n * P:(n + 1) * P]
                        pe.matmul(psum[:, k % 4, :], w_hi, xt_hi[:, kc], start=(kc == 0), stop=False)
                        pe.matmul(psum[:, k % 4, :], w_hi, xt_lo[:, kc], start=False, stop=False)
                        mm = pe.matmul(psum[:, k % 4, :], w_lo, xt_hi[:, kc], start=False, stop=(kc == KC - 1))
                    mm.then_inc(win_done, 1)

            def gates(t):
                for n in range(HC):
                    if n == 0:
                        pe.wait_ge(xh_done, HC * (t + 1))
                    if n >= 4:
                        pe.wait_ge(tanh_done, 2 * (HC * t + n - 3))
                    pe.matmul(psum[:, n % 4, :], wgate[:, n], xh[:, n // KC, n % KC],
                              start=True, stop=True).then_inc(gate_mm_done, 1)

            def out_project(t):
                for j in range(G):
                    if j == 0:
                        pe.wait_ge(h_done, 2 * KC * (t + 1))
                    bank = psum[:, OUT0 + j, :]
                    pe.matmul(bank, ones_row[:], bout_hi[:], start=True, stop=False)
                    pe.matmul(bank, ones_row[:], bout_lo[:], start=False, stop=False)
                    for k in range(HC):
                        mm = pe.matmul(bank, h[:, k // KC, k % KC, j * P:(j + 1) * P], wout[:, k],
                                       start=False, stop=(k == HC - 1))
                    mm.then_inc(out_done, 1)

            pe.wait_ge(consts_loaded, 16 * 7)
            transposes(0)
            pe.wait_ge(win_hi_done, KC)
            pe.wait_ge(win_lo_done, KC)
            project(0)
            gates(0)

            def step(t):
                if not last(t):
                    transposes(t + 1)
                if not first(t):
                    out_project(t - 1)
                if not last(t):
                    project(t + 1)
                    gates(t + 1)
                if first(t):
                    pe.wait_ge(wout_loaded, 16)
                    pe.wait_ge(dve_consts, 5)

            steps(pe, step)
            out_project(LAST)

        @block.scalar
        def _(act):
            act.wait_ge(win_loaded, 16)
            hw = h[:].rearrange("p a c t -> p (a c t)").rearrange("p (k n) -> p k n", k=KC)
            for kc in range(KC):
                act.activation(win_hi[:, kc], hw[:, kc], ACT.Copy).then_inc(win_hi_done, 1)
            act.wait_ge(consts_loaded, 16 * 7)
            act.activation(sp[:, 0], a_real[:], ACT.Abs).then_inc(act_small, 1)
            act.activation(bout_hi[:], bout_row[:], ACT.Copy).then_inc(act_small, 1)
            act.wait_ge(act_small, 2)
            act.activation(sp[:, 1], sp[:, 0], ACT.Exp, scale=-1.0).then_inc(act_small, 1)

            def xt_high(t):
                for j in range(G):
                    act.wait_ge(transposed, G * t + j + 1)
                    if j == 0:
                        wait(act, win_done, HC * t)
                    act.activation(xt_hi[:, :, j * P:(j + 1) * P],
                                   psum[:, j % 2, :].rearrange("p (c q) -> p c q", c=KC),
                                   ACT.Copy).then_inc(xt_hi_done, 1)

            def xh_evacuate(t):
                for k, n in enumerate((0, 4, 1, 5, 2, 6, 3, 7)):
                    act.wait_ge(win_done, HC * t + k + 1)
                    wait(act, fwd_done, 2 * (KC * (t - 1) + k // 2 + 1))
                    act.activation(xh[:, n // KC, n % KC], psum[:, k % 4, :], ACT.Identity,
                                   bias=b_in[:, n:n + 1]).then_inc(xh_done, 1)

            def tanhs(t):
                for n in range(HC):
                    act.wait_ge(gate_mm_done, HC * t + n + 1)
                    wait(act, gain_done, KC * (t - 1) + n // 2 + 1)
                    wait(act, mag2_done, KC * t)
                    to = slice(64 * (n % 2), 64 * (n % 2) + 64)
                    act.activation(tanh_x[to, n // 2], psum[0:64, n % 4, :], ACT.Tanh,
                                   bias=b_gate[0:64, n:n + 1], scale=0.5).then_inc(tanh_done, 1)
                    act.activation(tanh_a[to, n // 2], psum[64:128, n % 4, :], ACT.Tanh,
                                   bias=b_gate[64:128, n:n + 1], scale=0.5).then_inc(tanh_done, 1)

            def exps(t):
                for c in range(KC):
                    act.wait_ge(tanh_done, 2 * HC * t + 4 * (c + 1))
                    wait(act, gsin_done, 2 * KC * t)
                    act.activation(gain[:, c], tanh_a[:, c], ACT.Exp, bias=mag2_k[:, c:c + 1],
                                   scale=mag2_k[:, c:c + 1]).then_inc(mag2_done, 1)
                for c in range(KC):
                    wait(act, scan_done, 2 * (KC * (t - 1) + c + 1))
                    act.activation(mag[:, c], tanh_a[:, c], ACT.Exp, bias=mag_k[:, c:c + 1],
                                   scale=mag_k[:, c:c + 1]).then_inc(mag_done, 1)
                for c in range(KC):
                    act.wait_ge(z_done, KC * t + c + 1)
                    act.activation(gain[:, c], gain[:, c], ACT.Ln, scale=-1.0).then_inc(log_done, 1)
                for c in range(KC):
                    act.wait_ge(log_done, KC * t + c + 1)
                    act.activation(gain[:, c], gain[:, c], ACT.Exp, bias=ln_half[:, 0:1],
                                   scale=0.5).then_inc(norm_done, 1)

            def sines(t):
                for c in range(KC):
                    act.wait_ge(frac_done, KC * t + c + 1)
                    wait(act, back_mul_done, 2 * (KC * (t - 1) + c + 1))
                    act.activation(sin[:, c], frac[:, c], ACT.Sin, scale=-TWO_PI_SAFE).then_inc(sin_done, 1)
                    act.activation(cos[:, c], frac[:, c], ACT.Abs).then_inc(abs_done, 1)
                for c in range(KC):
                    act.wait_ge(abs_done, KC * t + c + 1)
                    act.activation(cos[:, c], cos[:, c], ACT.Sin, bias=halfpi[:, 0:1],
                                   scale=-TWO_PI_SAFE).then_inc(cos_done, 1)

            def y_normalise(t):
                for j in range(G):
                    act.wait_ge(y_scaled, G * t + j + 1)
                    act.activation(psum[:, OUT0 + j, :], psum[:, OUT0 + j, :], ACT.Identity,
                                   bias=y_sc[:, 1, j:j + 1], scale=y_sc[:, 0, j:j + 1]).then_inc(y_normed, 1)

            xt_high(0)
            act.wait_ge(dve_consts, 5)
            xh_evacuate(0)
            tanhs(0)

            def step(t):
                if not last(t):
                    xt_high(t + 1)
                exps(t)
                sines(t)
                if not first(t):
                    y_normalise(t - 1)
                if not last(t):
                    xh_evacuate(t + 1)
                    tanhs(t + 1)

            steps(act, step)
            y_normalise(LAST)

        @block.vector
        def _(dve):
            def x_statistics(t):
                dve.wait_ge(xin_loaded, 16 * (t + 1))
                wait(dve, x_stats, G * t)
                wait(dve, xn_done, G * t)
                for j in range(G):
                    dve.bn_stats(x_bn[:, j], x_in[:, j]).then_inc(x_bn_done, 1)
                for j in range(G):
                    dve.wait_ge(x_bn_done, G * t + j + 1)
                    after_wait(dve)
                    dve.bn_aggr(x_mv[:, j], x_bn[:, j]).then_inc(x_stats, 1)

            def xt_low(t):
                for j in range(G):
                    dve.wait_ge(xt_hi_done, G * t + j + 1)
                    at = slice(j * P, (j + 1) * P)
                    dve.tensor_tensor(xt_lo[:, :, at], psum[:, j % 2, :].rearrange("p (c q) -> p c q", c=KC),
                                      xt_hi[:, :, at].bitcast(F32), ALU.subtract).then_inc(xt_lo_done, 1)

            dve.memset(ones[:], 1.0).then_inc(dve_consts, 1)
            dve.memset(halfpi[:], math.pi / 2).then_inc(dve_consts, 1)
            dve.memset(ln_half[:], math.log(0.5)).then_inc(dve_consts, 1)
            dve.memset(carry[:], 0.0).then_inc(carry_done, 1)
            dve.memset(keep[:], 1.0).then_inc(dve_small, 1)
            dve.wait_ge(dve_small, 1)
            dve.memset(keep[:, 0:NT + 1:TPB], 0.0).then_inc(dve_small, 1)
            x_statistics(0)
            dve.wait_ge(dve_consts, 1)
            dve.tensor_copy(ones_row[:], ones[0:1, 0:P]).then_inc(dve_consts, 1)
            hw = h[:].rearrange("p a c t -> p (a c t)").rearrange("p (k n) -> p k n", k=KC)
            for kc in range(KC):
                dve.wait_ge(win_hi_done, kc + 1)
                dve.tensor_tensor(win_lo[:, kc], hw[:, kc], win_hi[:, kc].bitcast(F32),
                                  ALU.subtract).then_inc(win_lo_done, 1)
            small = [2]

            def link(ins):
                small[0] += 1
                ins.then_inc(dve_small, 1)
                dve.wait_ge(dve_small, small[0])

            dve.wait_ge(act_small, 3)
            link(dve.tensor_tensor(bout_lo[:], bout_row[:], bout_hi[:].bitcast(F32), ALU.subtract))
            link(dve.tensor_scalar(b_gate[:], b_gate[:], 0.5, None, ALU.mult))
            link(dve.tensor_scalar(half_turn[:], a_imag[:], 1 / (4 * math.pi), None, ALU.mult))
            link(dve.tensor_scalar(sp[:, 2], sp[:, 1], 2.0, None, ALU.add))
            link(dve.reciprocal(sp[:, 3], sp[:, 2]))
            link(dve.tensor_tensor(sp[:, 3], sp[:, 3], sp[:, 1], ALU.mult))
            link(dve.tensor_tensor(sp[:, 4], sp[:, 3], sp[:, 3], ALU.mult))
            link(dve.tensor_scalar(sp[:, 5], sp[:, 4], 1 / 17, 1 / 15, ALU.mult, ALU.add))
            for k in (13, 11, 9, 7, 5, 3, 1):
                link(dve.tensor_tensor(sp[:, 5], sp[:, 5], sp[:, 4], ALU.mult))
                link(dve.tensor_scalar(sp[:, 5], sp[:, 5], 1 / k, None, ALU.add))
            link(dve.tensor_tensor(sp[:, 5], sp[:, 5], sp[:, 3], ALU.mult))
            link(dve.tensor_scalar(sp[:, 2], a_real[:], 0.0, 0.5, ALU.max, ALU.mult))
            link(dve.tensor_tensor(sp[:, 5], sp[:, 5], sp[:, 2], ALU.add))
            link(dve.tensor_scalar(mag_k[:], sp[:, 5], LOG_A_SCALE, None, ALU.mult))
            dve.tensor_scalar(mag2_k[:], sp[:, 5], 2 * LOG_A_SCALE, None, ALU.mult).then_inc(dve_consts, 1)
            x_statistics(1)
            xt_low(0)

            def phases(t):
                for c in range(KC):
                    dve.wait_ge(tanh_done, 2 * HC * t + 4 * (c + 1))
                    wait(dve, fwd_mul_done, 2 * (KC * (t - 1) + c + 1))
                    dve.tensor_scalar(turns[:, c], tanh_a[:, c], half_turn[:, c:c + 1], half_turn[:, c:c + 1],
                                      ALU.mult, ALU.add).then_inc(inc_done, 1)
                for c in range(KC):
                    dve.wait_ge(inc_done, KC * t + c + 1)
                    dve.tensor_tensor_scan(turns[:, c], ones[:], turns[:, c], 0.0,
                                           ALU.mult, ALU.add).then_inc(turns_done, 1)
                for c in range(KC):
                    dve.wait_ge(turns_done, KC * t + c + 1)
                    dve.tensor_scalar(frac[:, c], turns[:, c], MAGIC, None, ALU.add).then_inc(round_done, 1)
                for c in range(KC):
                    dve.wait_ge(round_done, KC * t + c + 1)
                    dve.scalar_tensor_tensor(frac[:, c], frac[:, c], MAGIC, turns[:, c],
                                             ALU.subtract, ALU.subtract).then_inc(frac_done, 1)

            def norms(t):
                for c in range(KC):
                    dve.wait_ge(mag2_done, KC * t + c + 1)
                    dve.tensor_scalar(gain[:, c], gain[:, c], 1.0, -1e-6, ALU.subtract,
                                      ALU.min).then_inc(z_done, 1)

            def gains(t):
                for c in range(KC):
                    dve.wait_ge(norm_done, KC * t + c + 1)
                    dve.scalar_tensor_tensor(gain[:, c], tanh_x[:, c], 1.0, gain[:, c],
                                             ALU.add, ALU.mult).then_inc(gain_done, 1)
                for c in range(KC):
                    dve.wait_ge(gain_done, KC * t + c + 1)
                    dve.wait_ge(sin_done, KC * t + c + 1)
                    dve.tensor_tensor(turns[:, c], gain[:, c], sin[:, c], ALU.mult).then_inc(gsin_done, 1)
                    dve.wait_ge(cos_done, KC * t + c + 1)
                    dve.tensor_tensor(frac[:, c], gain[:, c], cos[:, c], ALU.mult).then_inc(gsin_done, 1)

            def both(plane, c):
                return plane[:, c:c + 1, :].to_broadcast([P, 2, T])

            def rotate_products(t):
                for c in range(KC):
                    dve.wait_ge(gsin_done, 2 * (KC * t + c + 1))
                    wait(dve, h_done, 2 * (KC * (t - 1) + c + 1))
                    dve.tensor_tensor(cross[:, :, c], xh[:, :, c], both(turns, c), ALU.mult).then_inc(fwd_mul_done, 1)
                    dve.wait_ge(fwd_mul_done, 2 * (KC * t + c) + 1)
                    dve.tensor_tensor(xh[:, :, c], xh[:, :, c], both(frac, c), ALU.mult).then_inc(fwd_mul_done, 1)

            def recur(t):
                wait(dve, out_done, G * t)
                if first(t):
                    dve.wait_ge(win_lo_done, KC)
                for c in range(KC):
                    dve.wait_ge(fwd_mul_done, 2 * (KC * t + c + 1))
                    dve.tensor_tensor(h[:, 0, c], xh[:, 0, c], cross[:, 1, c], ALU.add).then_inc(fwd_done, 1)
                    dve.tensor_tensor(h[:, 1, c], xh[:, 1, c], cross[:, 0, c], ALU.subtract).then_inc(fwd_done, 1)
                dve.wait_ge(carry_done, t + 1)
                dve.wait_ge(mag_done, KC * (t + 1))
                for c in range(KC):
                    for ri in range(2):
                        dve.wait_ge(fwd_done, 2 * (KC * t + c) + ri + 1)
                        dve.tensor_tensor_scan(h[:, ri, c], mag[:, c], h[:, ri, c], carry[:, ri, c:c + 1],
                                               ALU.mult, ALU.add).then_inc(scan_done, 1)
                for c in range(KC):
                    dve.wait_ge(scan_done, 2 * (KC * t + c + 1))
                    dve.tensor_tensor(cross[:, :, c], h[:, :, c], both(sin, c), ALU.mult).then_inc(back_mul_done, 1)
                    dve.wait_ge(back_mul_done, 2 * (KC * t + c) + 1)
                    dve.tensor_tensor(h[:, :, c], h[:, :, c], both(cos, c), ALU.mult).then_inc(back_mul_done, 1)
                for c in range(KC):
                    dve.wait_ge(back_mul_done, 2 * (KC * t + c + 1))
                    dve.tensor_tensor(h[:, 0, c], h[:, 0, c], cross[:, 1, c], ALU.subtract).then_inc(h_done, 1)
                    dve.tensor_tensor(h[:, 1, c], h[:, 1, c], cross[:, 0, c], ALU.add).then_inc(h_done, 1)
                dve.wait_ge(h_done, 2 * KC * (t + 1))
                at = slice(t + 1, t + 2) if isinstance(t, int) else bass.ds(t + 1, 1)
                dve.tensor_scalar(carry[:], h[:, :, :, T - 1], keep[:, at], None, ALU.mult).then_inc(carry_done, 1)

            def y_stat(t, j):
                dve.wait_ge(out_done, G * t + j + 1)
                dve.bn_stats(y_bn[:, j], psum[:, OUT0 + j, :]).then_inc(y_bn_done, 1)
                dve.wait_ge(y_bn_done, G * t + j + 1)
                after_wait(dve)
                dve.bn_aggr(y_mv[:, j], y_bn[:, j]).then_inc(y_stats, 1)

            def y_add(t, j):
                dve.wait_ge(y_normed, G * t + j + 1)
                dve.wait_ge(xres_loaded, 16 * (t + 1))
                dve.tensor_tensor(x_res[:, j], psum[:, OUT0 + j, :], x_res[:, j], ALU.add).then_inc(x1_ready, 1)

            def finish(t):
                for j in range(G):
                    y_stat(t, j)
                    if j > 0:
                        y_add(t, j - 1)
                y_add(t, G - 1)

            def step(t):
                if not last(t):
                    xt_low(t + 1)
                phases(t)
                norms(t)
                gains(t)
                rotate_products(t)
                if not first(t):
                    finish(t - 1)
                if not (isinstance(t, int) and t >= NT - 2):
                    x_statistics(t + 2)
                recur(t)

            step(0)
            with dve.Fori(0, (NT - 2) // 2 - 1) as i:
                for u in range(2):
                    step(2 * i + (1 + u))
            step(NT - 3)
            step(NT - 2)
            step(LAST)
            finish(LAST)


def phase_b(nc, d, NQ=NE):
    with ExitStack() as ctx:
        def sb(name, shape, dt=F32):
            return ctx.enter_context(nc.sbuf_tensor(name, shape, dt))

        def sem(name):
            return ctx.enter_context(nc.semaphore(name))

        sw1_hi, sw1_lo = sb("sw1_hi", [P, KC, HS], F32R), sb("sw1_lo", [P, KC, HS], F32R)
        sw3_hi, sw3_lo = sb("sw3_hi", [P, KC, HS], F32R), sb("sw3_lo", [P, KC, HS], F32R)
        sw2_hi, sw2_lo = sb("sw2_hi", [P, HS // P, D], F32R), sb("sw2_lo", [P, HS // P, D], F32R)
        w1_hi, w1_lo = sb("w1_hi", [P, 2, KC, HR], F32R), sb("w1_lo", [P, 2, KC, HR], F32R)
        w2_hi, w2_lo = sb("w2_hi", [P, 2, KC, D], F32R), sb("w2_lo", [P, 2, KC, D], F32R)
        stage = sb("stage", [P, RING, D])
        xt_hi, xt_lo = sb("fx_hi", [P, KC, T], F32R), sb("fx_lo", [P, KC, T], F32R)
        x1 = sb("x1_tile", [P, 2, G, D])
        xn = sb("fxn", [P, 2, D])
        gate = sb("gate", [P, T])
        hid_hi, hid_lo = sb("hid_hi", [P, 2, T], F32R), sb("hid_lo", [P, 2, T], F32R)
        bias = sb("bias", [P, D])
        brow = sb("brow", [3, D])
        bsel = sb("bsel", [3, P])
        ident = sb("f_ident", [P, P])
        b_s1, b_s3 = sb("b_s1", [P, HS // P]), sb("b_s3", [P, HS // P])
        b_r1 = sb("b_r1", [P, (NE + 1) * KC])
        neg_half = sb("f_neg_half", [P, G])
        x_bn, x_mv, x_sc = sb("fx_bn", [P, G, 6]), sb("fx_mv", [P, G, 2]), sb("fx_sc", [P, 2, G])
        y_bn, y_mv, y_sc = sb("fy_bn", [P, G, 6]), sb("fy_mv", [P, G, 2]), sb("fy_sc", [P, 2, G])
        psum = ctx.enter_context(nc.psum_tensor("psum_b", [P, 8, 512], F32))
        HID0, OUT0 = 2, 4

        consts_loaded = sem("f_consts_loaded")
        pool_consts = sem("f_pool_consts")
        x1_loaded = [sem(f"f_x1_loaded{k}") for k in range(2)]
        x2_stored = [sem(f"f_x2_stored{k}") for k in range(2)]
        piece_loaded = [sem(f"f_piece_loaded{k}") for k in range(RING)]
        brow_loaded = sem("f_brow_loaded")
        bias_mm_done = sem("f_bias_mm_done")
        bias_done = sem("f_bias_done")
        piece_hi_done = sem("f_piece_hi_done")
        piece_lo_done = sem("f_piece_lo_done")
        x_bn_done = sem("f_x_bn_done")
        x_stats = sem("f_x_stats")
        x_small = sem("f_x_small")
        xn_done = sem("f_xn_done")
        transposed = sem("f_transposed")
        xt_hi_done = sem("f_xt_hi_done")
        xt_lo_done = sem("f_xt_lo_done")
        hid_mm_done = sem("f_hid_mm_done")
        act_done = sem("f_act_done")
        prod_done = sem("f_prod_done")
        hid_hi_done = sem("f_hid_hi_done")
        hid_lo_done = sem("f_hid_lo_done")
        out_unit_done = sem("f_out_unit_done")
        out_done = sem("f_out_done")
        y_biased = sem("f_y_biased")
        y_bn_done = sem("f_y_bn_done")
        y_stats = sem("f_y_stats")
        y_small = sem("f_y_small")
        y_scaled = sem("f_y_scaled")
        y_normed = sem("f_y_normed")
        x2_ready = sem("f_x2_ready")

        OLD, SHARED, NEW = range(3)
        kinds = [OLD] * KC + [SHARED] * (HS // P) + [NEW] * KC
        UN = len(kinds)
        starts = [sum(2 if x == SHARED else 1 for x in kinds[:k]) for k in range(UN + 1)]
        HM = starts[UN]

        by_class = "(g p r) d -> r p g d"
        x1_rows = d["x1"].rearrange(by_class, p=P, r=NE)
        out_rows = d["out"].rearrange(by_class, p=P, r=NE)

        def rows_of(rows, q, hf):
            at = slice(hf * G, (hf + 1) * G)
            if isinstance(q, int):
                return rows[5 * q % NE, :, at]
            return rows[bass.ds(5 * q % NE, 1), :, at].rearrange("o p g d -> p (o g) d")

        def steps(eng, step):
            for hf in range(2):
                step(hf, 0, hf, 0)
            if NQ > 2:
                with eng.Fori(0, (NQ - 2) // 2) as i:
                    for v in range(2):
                        for hf in range(2):
                            q = 2 * i + (1 + v)
                            step(4 * i + (2 * (1 + v) + hf), q, hf, (1 + v) % 2)
            for hf in range(2):
                step(2 * (NQ - 1) + hf, NQ - 1, hf, (NQ - 1) % 2)

        def is_last(m):
            return isinstance(m, int) and m == 2 * NQ - 1

        def first(m):
            return isinstance(m, int) and m == 0

        def expert_pieces(slot):
            return ([(w1_hi[:, slot, k], w1_lo[:, slot, k], 1.0) for k in range(KC)]
                    + [(w2_hi[:, slot, k], w2_lo[:, slot, k], 0.5) for k in range(KC)])

        def shared_pieces(half):
            at = slice(half * 512, (half + 1) * 512)
            return ([(sw1_hi[:, k, at], sw1_lo[:, k, at], 1.0) for k in range(KC)]
                    + [(sw3_hi[:, k, at], sw3_lo[:, k, at], 1.0) for k in range(KC)]
                    + [(sw2_hi[:, k], sw2_lo[:, k], 1.0) for k in range(half * KC, half * KC + KC)])

        FIRST = expert_pieces(0) + shared_pieces(0) + shared_pieces(1) + expert_pieces(1)
        NF = len(FIRST)

        def pieces_after(m, q, hf, par, k):
            if first(m):
                cuts = [0, 8, 11, 14, 17, 20, 23, 26, 29, 32, 34, 36, 38, 40, 40, 40, 40, 40]
                return [(n, FIRST[n]) for n in range(cuts[k + 1], cuts[k + 2])]
            more = not (isinstance(q, int) and q == NQ - 1)
            if hf == 1 and more and 5 <= k < 5 + 8:
                return [(8 * q + (NF + k - 5), expert_pieces(par)[k - 5])]
            return []

        block = ctx.enter_context(nc.Block())

        @block.sync
        def _(sp):
            def load_piece(n, slot, src):
                sp.dma_start(stage[:, slot], src).then_inc(piece_loaded[slot], 16)

            w1d = d["w1"].rearrange("e (k p) n -> e k p n", p=P)
            w2d = d["w2"].rearrange("e (k p) n -> e k p n", p=P)

            def of_expert(j, k):
                src, kk = (w1d, k) if k < KC else (w2d, k - KC)
                if isinstance(j, int):
                    return src[(NE - 1) * j % NE, kk]
                return src[bass.ds((NE - 1) * j % NE, 1), kk].rearrange("e p n -> p (e n)")

            def of_shared(half, k):
                if k < 2 * KC:
                    w = d["sw1"] if k < KC else d["sw3"]
                    return w.rearrange("(k p) n -> k p n", p=P)[k % KC, :, half * 512:(half + 1) * 512]
                return d["sw2"].rearrange("(k p) n -> k p n", p=P)[half * KC + k - 2 * KC]

            sources = ([of_expert(0, k) for k in range(8)] + [of_shared(0, k) for k in range(12)]
                       + [of_shared(1, k) for k in range(12)] + [of_expert(1, k) for k in range(8)])
            sp.dma_start(x1[:, 0], rows_of(x1_rows, 0, 0)).then_inc(x1_loaded[0], 16)
            for dst, src in ((ident, "ident"), (bsel, "bsel"), (b_s1, "b_s1"), (b_s3, "b_s3"), (b_r1, "b_r1")):
                sp.dma_start(dst[:], d[src]).then_inc(consts_loaded, 16)
            sp.dma_start(brow[0:1, :], d["b_s2"]).then_inc(consts_loaded, 16)
            sp.dma_start(brow[1:3, :], d["b_r2"][0:2]).then_inc(brow_loaded, 16)
            for n in range(NF):
                wait(sp, piece_lo_done, n - RING + 1)
                load_piece(n, n % RING, sources[n])
                if n == 7:
                    sp.dma_start(x1[:, 1], rows_of(x1_rows, 0, 1)).then_inc(x1_loaded[1], 16)

            def step(m, q, hf, par):
                if not first(m):
                    sp.wait_ge(x2_ready, G * m)
                    after_wait(sp)
                    prev_q, prev_hf = (q, 0) if hf == 1 else (q - 1, 1)
                    sp.dma_start(rows_of(out_rows, prev_q, prev_hf), x1[:, 1 - hf]).then_inc(x2_stored[1 - hf], 16)
                    if not is_last(m):
                        n_stored = q + 1 if hf == 1 else q
                        sp.wait_ge(x2_stored[1 - hf], 16 * n_stored)
                        after_wait(sp)
                        next_q, next_hf = (q + 1, 0) if hf == 1 else (q, 1)
                        sp.dma_start(x1[:, next_hf], rows_of(x1_rows, next_q, next_hf)).then_inc(
                            x1_loaded[next_hf], 16)
                if hf == 0 and not first(m):
                    sp.wait_ge(bias_mm_done, q)
                    after_wait(sp)
                    rows = d["b_r2"][q:q + 2] if isinstance(q, int) else d["b_r2"][bass.ds(q, 2)]
                    sp.dma_start(brow[1:3, :], rows).then_inc(brow_loaded, 16)
                if hf == 1 and not (isinstance(q, int) and q == NQ - 1):
                    for k in range(8):
                        sp.wait_ge(piece_lo_done, 8 * q + (NF + k - RING + 1))
                        after_wait(sp)
                        load_piece(None, k % RING, of_expert(q + 2, k))

            steps(sp, step)
            sp.wait_ge(x2_ready, G * 2 * NQ)
            sp.dma_start(rows_of(out_rows, NQ - 1, 1), x1[:, 1]).then_inc(x2_stored[1], 16)
            for k in range(2):
                sp.wait_ge(x2_stored[k], 16 * NQ)

        @block.gpsimd
        def _(pool):
            pool.memset(neg_half[:], -0.5).then_inc(pool_consts, 1)
            pool.wait_ge(pool_consts, 1)

            def scales(mv, sc, small, n, done, eps):
                after_wait(pool)
                pool.tensor_scalar(sc[:, 0], mv[:, :, 1], eps, 1.0, ALU.add, ALU.mult).then_inc(small, 1)
                pool.tensor_scalar(sc[:, 1], mv[:, :, 0], -1.0, 0.0, ALU.mult, ALU.add).then_inc(small, 1)
                pool.wait_ge(small, n + 2)
                w = sc.shape[-1]
                pool.tensor_tensor(sc[:, 0], sc[:, 0], neg_half[:, 0:w], ALU.pow).then_inc(small, 1)
                pool.wait_ge(small, n + 3)
                pool.tensor_tensor(sc[:, 1], sc[:, 1], sc[:, 0], ALU.mult).then_inc(done, 1)

            def norm_x(m, hf):
                pool.wait_ge(x_stats, G * (m + 1))
                wait(pool, xn_done, G * m)
                scales(x_mv[:], x_sc[:], x_small, 4 * m, x_small, EPS)
                pool.wait_ge(x_small, 4 * m + 4)
                for j in range(G):
                    wait(pool, transposed, G * m + j - 1)
                    after_wait(pool)
                    pool.tensor_scalar(xn[:, j % 2], x1[:, hf, j], x_sc[:, 0, j:j + 1], x_sc[:, 1, j:j + 1],
                                       ALU.mult, ALU.add).then_inc(xn_done, 1)

            def norm_y(m):
                for j in range(G):
                    pool.wait_ge(y_stats, G * m + j + 1)
                    scales(y_mv[:, j:j + 1], y_sc[:, :, j:j + 1], y_small, 3 * (G * m + j), y_scaled, 4 * EPS)

            norm_x(0, 0)

            def step(m, q, hf, par):
                if not first(m):
                    norm_y(m - 1)
                if not is_last(m):
                    norm_x(m + 1, 1 - hf)

            steps(pool, step)
            norm_y(2 * NQ - 1)

        @block.tensor
        def _(pe):
            def transposes(m, js):
                for j in js:
                    pe.wait_ge(xn_done, G * m + j + 1)
                    wait(pe, xt_lo_done, G * m + j - 1)
                    for c in range(KC):
                        mm = pe.transpose(psum[:, j % 2, c * P:(c + 1) * P], xn[:, j % 2, c * P:(c + 1) * P],
                                          ident[:])
                    mm.then_inc(transposed, 1)

            def split_product(bank, w_hi, w_lo, at):
                for kc in range(KC):
                    pe.matmul(bank, w_hi[:, kc, at], xt_hi[:, kc], start=(kc == 0), stop=False)
                    pe.matmul(bank, w_hi[:, kc, at], xt_lo[:, kc], start=False, stop=False)
                    mm = pe.matmul(bank, w_lo[:, kc, at], xt_hi[:, kc], start=False, stop=(kc == KC - 1))
                mm.then_inc(hid_mm_done, 1)

            def hidden(m, par, k):
                kind = kinds[k]
                if kind == SHARED:
                    at = slice((k - KC) * P, (k - KC + 1) * P)
                    if k == KC:
                        pe.wait_ge(hid_lo_done, UN * m + k - 1)
                    else:
                        pe.wait_ge(act_done, UN * m + k)
                    split_product(psum[:, HID0, :], sw1_hi, sw1_lo, at)
                    pe.wait_ge(hid_lo_done, UN * m + k)
                    split_product(psum[:, HID0 + 1, :], sw3_hi, sw3_lo, at)
                    return
                c = k if kind == OLD else k - (UN - KC)
                slot = par if kind == OLD else 1 - par
                if kind == NEW and c == 0:
                    pe.wait_ge(act_done, UN * m + k)
                elif kind == NEW and c == 1:
                    pe.wait_ge(hid_lo_done, UN * m + k - 1)
                else:
                    wait(pe, hid_lo_done, UN * m + k - 1)
                split_product(psum[:, HID0 + c % 2, :], w1_hi[:, slot], w1_lo[:, slot],
                              slice(c * P, (c + 1) * P))

            def output(m, par, k):
                kind = kinds[k]
                if kind == SHARED:
                    w_hi, w_lo = sw2_hi[:, k - KC], sw2_lo[:, k - KC]
                else:
                    c = k if kind == OLD else k - (UN - KC)
                    slot = par if kind == OLD else 1 - par
                    w_hi, w_lo = w2_hi[:, slot, c], w2_lo[:, slot, c]
                pe.wait_ge(hid_lo_done, UN * m + k + 1)
                for j in range(G):
                    if k == 0:
                        wait(pe, x2_ready, G * (m - 1) + j + 1)
                    at = slice(j * P, (j + 1) * P)
                    bank = psum[:, OUT0 + j, :]
                    pe.matmul(bank, hid_hi[:, k % 2, at], w_hi, start=(k == 0), stop=False)
                    pe.matmul(bank, hid_hi[:, k % 2, at], w_lo, start=False, stop=False)
                    mm = pe.matmul(bank, hid_lo[:, k % 2, at], w_hi, start=False, stop=(k == UN - 1))
                    if k == UN - 1:
                        mm.then_inc(out_done, 1)
                    elif j == G - 1:
                        mm.then_inc(out_unit_done, 1)

            def bias_product(q):
                pe.wait_ge(brow_loaded, 16 * (q + 1))
                pe.matmul(psum[:, 0, :], bsel[:], brow[:], start=True, stop=True).then_inc(bias_mm_done, 1)

            pe.wait_ge(consts_loaded, 16 * 6)
            transposes(0, range(G))

            def step(m, q, hf, par):
                pe.wait_ge(xt_lo_done, G * (m + 1))
                for k in range(UN):
                    if first(m) and k in (0, 4, 8, 12):
                        pe.wait_ge(piece_lo_done, {0: 8, 4: 20, 8: 32, 12: 40}[k])
                    elif k == UN - KC and hf == 0 and not first(m):
                        pe.wait_ge(piece_lo_done, 8 * q + NF)
                    if k == UN - 1 and not is_last(m):
                        if hf == 0:
                            pe.wait_ge(bias_done, q + 1)
                        transposes(m + 1, (0, 1))
                    hidden(m, par, k)
                    if k > 0:
                        output(m, par, k - 1)
                    if k == 7 and hf == 0:
                        bias_product(q)
                if not is_last(m):
                    transposes(m + 1, (2, 3))
                output(m, par, UN - 1)

            steps(pe, step)

        @block.scalar
        def _(act):
            def xt_high(m, js):
                for j in js:
                    act.wait_ge(transposed, G * m + j + 1)
                    if j == 0:
                        wait(act, hid_mm_done, HM * m)
                    act.activation(xt_hi[:, :, j * P:(j + 1) * P],
                                   psum[:, j % 2, :].rearrange("p (c q) -> p c q", c=KC),
                                   ACT.Copy).then_inc(xt_hi_done, 1)

            def pieces_high(m, q, hf, par, k):
                for n, (w_hi, _, scale) in pieces_after(m, q, hf, par, k):
                    slot = n % RING if isinstance(n, int) else (k - 5) % RING
                    turn = n // RING if isinstance(n, int) else 2 * q + (NF + k - 5) // RING
                    act.wait_ge(piece_loaded[slot], 16 * (turn + 1))
                    if not first(m):
                        act.wait_ge(out_unit_done, (UN - 1) * m + KC)
                    act.activation(w_hi, stage[:, slot], ACT.Copy, scale=scale).then_inc(piece_hi_done, 1)

            def activate(m, q, k):
                kind = kinds[k]
                act.wait_ge(hid_mm_done, HM * m + starts[k] + 1)
                if kind == SHARED:
                    wait(act, prod_done, (HS // P) * m + k - KC)
                    act.activation(gate[:], psum[:, HID0, :], ACT.Silu,
                                   bias=b_s1[:, k - KC:k - KC + 1]).then_inc(act_done, 1)
                else:
                    c = k if kind == OLD else k - (UN - KC)
                    j = q if kind == OLD else q + 1
                    col = KC * j + c
                    at = slice(col, col + 1) if isinstance(col, int) else bass.ds(col, 1)
                    bank = psum[:, HID0 + c % 2, :]
                    after_wait(act)
                    act.activation(bank, bank, ACT.Gelu, bias=b_r1[:, at]).then_inc(act_done, 1)

            def hidden_high(m, k):
                kind = kinds[k]
                if kind == SHARED:
                    act.wait_ge(prod_done, (HS // P) * m + k - KC + 1)
                    bank = psum[:, HID0 + 1, :]
                else:
                    act.wait_ge(act_done, UN * m + k + 1)
                    bank = psum[:, HID0 + (k if kind == OLD else k - (UN - KC)) % 2, :]
                if k >= 2:
                    act.wait_ge(out_unit_done, (UN - 1) * m + k - 1)
                elif k == 1:
                    wait(act, out_done, G * m)
                else:
                    wait(act, out_unit_done, (UN - 1) * m)
                act.activation(hid_hi[:, k % 2], bank, ACT.Copy).then_inc(hid_hi_done, 1)

            def y_normalise(m, js):
                for j in js:
                    act.wait_ge(y_scaled, G * m + j + 1)
                    bank = psum[:, OUT0 + j, :]
                    act.activation(bank, bank, ACT.Identity, bias=y_sc[:, 1, j:j + 1],
                                   scale=y_sc[:, 0, j:j + 1]).then_inc(y_normed, 1)

            act.wait_ge(consts_loaded, 16 * 6)
            xt_high(0, range(G))
            pieces_high(0, 0, 0, 0, -1)

            def step(m, q, hf, par):
                if not first(m):
                    y_normalise(m - 1, (0, 1))
                for k in range(UN):
                    if k == UN - 1 and not is_last(m):
                        act.wait_ge(hid_mm_done, HM * (m + 1))
                        xt_high(m + 1, (0, 1))
                    activate(m, q, k)
                    hidden_high(m, k)
                    if k == 0 and not first(m):
                        y_normalise(m - 1, (2, 3))
                    pieces_high(m, q, hf, par, k)
                if not is_last(m):
                    xt_high(m + 1, (2, 3))

            steps(act, step)
            y_normalise(2 * NQ - 1, range(G))

        @block.vector
        def _(dve):
            def x_statistics(m, q, hf):
                dve.wait_ge(x1_loaded[hf], 16 * (q + 1))
                wait(dve, x_stats, G * m)
                wait(dve, xn_done, G * m)
                for j in range(G):
                    dve.bn_stats(x_bn[:, j], x1[:, hf, j]).then_inc(x_bn_done, 1)
                for j in range(G):
                    dve.wait_ge(x_bn_done, G * m + j + 1)
                    after_wait(dve)
                    dve.bn_aggr(x_mv[:, j], x_bn[:, j]).then_inc(x_stats, 1)

            def xt_low(m, js):
                for j in js:
                    dve.wait_ge(xt_hi_done, G * m + j + 1)
                    at = slice(j * P, (j + 1) * P)
                    dve.tensor_tensor(xt_lo[:, :, at], psum[:, j % 2, :].rearrange("p (c q) -> p c q", c=KC),
                                      xt_hi[:, :, at].bitcast(F32), ALU.subtract).then_inc(xt_lo_done, 1)

            def pieces_low(m, q, hf, par, k):
                for n, (w_hi, w_lo, scale) in pieces_after(m, q, hf, par, k):
                    slot = n % RING if isinstance(n, int) else (k - 5) % RING
                    dve.wait_ge(piece_hi_done, n + 1)
                    dve.scalar_tensor_tensor(w_lo, stage[:, slot], scale, w_hi.bitcast(F32), ALU.mult,
                                             ALU.subtract).then_inc(piece_lo_done, 1)

            def product(m, k):
                if kinds[k] != SHARED:
                    return
                bank = psum[:, HID0 + 1, :]
                dve.wait_ge(hid_mm_done, HM * m + starts[k] + 2)
                dve.wait_ge(act_done, UN * m + k + 1)
                dve.scalar_tensor_tensor(bank, bank, b_s3[:, k - KC:k - KC + 1], gate[:], ALU.add,
                                         ALU.mult).then_inc(prod_done, 1)

            def hidden_low(m, k):
                kind = kinds[k]
                bank = psum[:, HID0 + (1 if kind == SHARED else (k if kind == OLD else k - (UN - KC)) % 2), :]
                dve.wait_ge(hid_hi_done, UN * m + k + 1)
                dve.tensor_tensor(hid_lo[:, k % 2], bank, hid_hi[:, k % 2].bitcast(F32),
                                  ALU.subtract).then_inc(hid_lo_done, 1)

            def y_stat(m, j):
                bank = psum[:, OUT0 + j, :]
                dve.wait_ge(out_done, G * m + j + 1)
                dve.tensor_tensor(bank, bank, bias[:], ALU.add).then_inc(y_biased, 1)
                dve.wait_ge(y_biased, G * m + j + 1)
                dve.bn_stats(y_bn[:, j], bank).then_inc(y_bn_done, 1)
                dve.wait_ge(y_bn_done, G * m + j + 1)
                after_wait(dve)
                dve.bn_aggr(y_mv[:, j], y_bn[:, j]).then_inc(y_stats, 1)

            def y_add(m, hf, j):
                dve.wait_ge(y_normed, G * m + j + 1)
                dve.tensor_tensor(x1[:, hf, j], psum[:, OUT0 + j, :], x1[:, hf, j], ALU.add).then_inc(x2_ready, 1)

            dve.wait_ge(consts_loaded, 16 * 6)
            x_statistics(0, 0, 0)
            xt_low(0, range(G))
            pieces_low(0, 0, 0, 0, -1)

            def step(m, q, hf, par):
                prev = 1 - hf
                if not first(m):
                    y_stat(m - 1, 0)
                    y_stat(m - 1, 1)
                    y_add(m - 1, prev, 0)
                    y_stat(m - 1, 2)
                    y_add(m - 1, prev, 1)
                for k in range(UN):
                    if k == UN - 1 and not is_last(m):
                        xt_low(m + 1, (0, 1))
                    product(m, k)
                    hidden_low(m, k)
                    if k == 0 and not first(m):
                        y_stat(m - 1, 3)
                        y_add(m - 1, prev, 2)
                        y_add(m - 1, prev, 3)
                    pieces_low(m, q, hf, par, k)
                    if k == 8 and hf == 0:
                        dve.wait_ge(bias_mm_done, q + 1)
                        dve.tensor_copy(bias[:], psum[:, 0, :]).then_inc(bias_done, 1)
                        if first(m):
                            dve.wait_ge(bias_done, 1)
                    if k == 10 and not is_last(m):
                        x_statistics(m + 1, q if hf == 0 else q + 1, 1 - hf)
                if not is_last(m):
                    xt_low(m + 1, (2, 3))

            steps(dve, step)
            for j in range(G):
                if j == 0:
                    dve.wait_ge(bias_done, NQ)
                y_stat(2 * NQ - 1, j)
            for j in range(G):
                y_add(2 * NQ - 1, 1, j)



def lay_out(inputs):
    import numpy as np

    def rows(w):
        return np.ascontiguousarray(w.reshape(-1, P, w.shape[-1]).transpose(1, 0, 2))

    def cols(v):
        return np.ascontiguousarray(v.reshape(-1, P).T)

    a = {k.removeprefix("L0_"): np.asarray(v) for k, v in inputs.items()}
    gate_b = np.concatenate([a["attn_b_gx"].reshape(HC, 64), a["attn_b_ga"].reshape(HC, 64)], axis=1).T
    return {
        "x": np.ascontiguousarray(a["attn_x"].reshape(N, D)),
        "w_in": rows(a["attn_w_in"]),
        "b_in": cols(a["attn_b_in"]),
        "w_gate": np.ascontiguousarray(np.concatenate([a["attn_w_gx"], a["attn_w_ga"]], axis=2).transpose(1, 0, 2)),
        "b_gate": np.ascontiguousarray(gate_b),
        "a_real": cols(a["attn_a_real_param"]),
        "a_imag": cols(a["attn_a_imag_param"]),
        "w_out": rows(a["attn_w_out"]),
        "b_out": np.ascontiguousarray(a["attn_b_out"].reshape(1, D)),
        "ident": np.eye(P, dtype=np.float32),
        "sw1": a["ffn_sw1"], "sw3": a["ffn_sw3"], "sw2": a["ffn_sw2"], "w1": a["ffn_w1"], "w2": a["ffn_w2"],
        "b_s1": cols(a["ffn_sb1"]),
        "b_s3": cols(a["ffn_sb3"]),
        "b_s2": np.ascontiguousarray(a["ffn_sb2"].reshape(1, D)),
        "b_r1": cols(np.concatenate([a["ffn_b1"][-j % NE] for j in range(NE + 1)])),
        "b_r2": np.ascontiguousarray(np.stack([a["ffn_b2"][-j % NE] for j in range(NE + 1)])),
        "bsel": np.repeat(np.array([[1.0], [0.5], [0.5]], np.float32), P, axis=1),
    }


def sandwich(nc, d):
    d["x1"] = nc.dram_tensor("x1_rows", (N, D), F32).ap()
    phase_a(nc, d)
    phase_b(nc, d)


def kernel(**inputs):
    import concourse.bacc as bacc
    from concourse.bass_utils import run_bass_kernel_spmd

    nc = bacc.Bacc("TRN2", target_bir_lowering=False, num_devices=1, dynamic_dma_scratch_size=1024)
    arrays = {f"in_{k}": v for k, v in lay_out(inputs).items()}
    d = {k[3:]: nc.dram_tensor(k, v.shape, F32, kind="ExternalInput").ap() for k, v in arrays.items()}
    d["out"] = nc.dram_tensor("out_rows", (N, D), F32, kind="ExternalOutput").ap()
    sandwich(nc, d)
    r = run_bass_kernel_spmd(nc, [arrays], core_ids=[0])
    return r.results[0]["out_rows"].reshape(B, S, D)
```

```python
from contextlib import ExitStack
import math

import concourse.bass as bass
from concourse import mybir

F32 = mybir.dt.float32
F32R = mybir.dt.float32r
ALU = mybir.AluOpType
ACT = mybir.ActivationFunctionType

P = 128
B, S, D = 4, 2048, 512
N = B * S
DH = 1024
KC = D // P
HC = DH // P
T = 512
G = T // P
NT = N // T
TPB = S // T
NE = 8
EPS = 1e-5
MAGIC = 1.5 * 2 ** 23
TWO_PI = 2 * math.pi
LOG_A_SCALE = -8.0
TWO_PI_SAFE = 6.283185
HS = 1024
HR = 512
RING = 4


def wait(eng, sem, n):
    if isinstance(n, int) and n <= 0:
        return
    eng.wait_ge(sem, n)


def after_wait(eng):
    eng.nop(nofuse=True)


def phase_a(nc, d, NT=NT):
    with ExitStack() as ctx:
        def sb(name, shape, dt=F32):
            return ctx.enter_context(nc.sbuf_tensor(name, shape, dt))

        def sem(name):
            return ctx.enter_context(nc.semaphore(name))

        win_hi = sb("win_hi", [P, KC, DH], F32R)
        win_lo = sb("win_lo", [P, KC, DH], F32R)
        wgate = sb("wgate", [P, HC, P])
        wout = sb("wout", [P, HC, D])
        x_in = sb("x_in", [P, G, D])
        x_res = sb("x_res", [P, G, D])
        xn = sb("xn", [P, G, D])
        xt_hi = sb("xt_hi", [P, KC, T], F32R)
        xt_lo = sb("xt_lo", [P, KC, T], F32R)
        xh = sb("xh", [P, 2, KC, T])
        tanh_x = sb("tanh_x", [P, KC, T])
        tanh_a = sb("tanh_a", [P, KC, T])
        mag = sb("mag", [P, KC, T])
        gain = sb("gain", [P, KC, T])
        turns = sb("turns", [P, KC, T])
        frac = sb("frac", [P, KC, T])
        sin = sb("sin", [P, KC, T])
        cos = sb("cos", [P, KC, T])
        h = sb("h", [P, 2, KC, T])
        cross = sb("cross", [P, 2, KC, T])
        ones = sb("ones", [P, T])
        ident = sb("ident", [P, P])
        bout_raw = sb("bout_raw", [2, D])
        bout_hi = sb("bout_hi", [2, D], F32R)
        bout = sb("bout", [2, D], F32R)
        low_row = sb("low_row", [2, 1])
        ones_row = sb("ones_row", [2, P], F32R)
        b_in = sb("b_in", [P, HC])
        b_gate = sb("b_gate", [P, HC])
        a_real = sb("a_real", [P, KC])
        a_imag = sb("a_imag", [P, KC])
        half_turn = sb("half_turn", [P, KC])
        sp = sb("sp", [P, 6, KC])
        mag_k = sb("mag_k", [P, KC])
        mag2_k = sb("mag2_k", [P, KC])
        halfpi = sb("halfpi", [P, 1])
        keep = sb("keep", [P, NT + 1])
        carry = sb("carry", [P, 2, KC])
        neg_half = sb("neg_half", [P, G])
        x_bn = sb("x_bn", [P, G, 6])
        x_mv = sb("x_mv", [P, G, 2])
        x_sc = sb("x_sc", [P, 2, G])
        y_bn = sb("y_bn", [P, G, 6])
        y_mv = sb("y_mv", [P, G, 2])
        y_sc = sb("y_sc", [P, 2, G])
        psum = ctx.enter_context(nc.psum_tensor("psum_a", [P, 8, 512], F32))
        OUT0 = 4

        consts_loaded = sem("consts_loaded")
        win_loaded = sem("win_loaded")
        wout_loaded = sem("wout_loaded")
        win_hi_done = sem("win_hi_done")
        win_lo_done = sem("win_lo_done")
        pool_consts = sem("pool_consts")
        dve_consts = sem("dve_consts")
        dve_small = sem("dve_small")
        act_small = sem("act_small")
        xin_loaded = sem("xin_loaded")
        xres_loaded = sem("xres_loaded")
        x1_stored = sem("x1_stored")
        x_stats = sem("x_stats")
        x_bn_done = sem("x_bn_done")
        xn_done = sem("xn_done")
        x_small = sem("x_small")
        y_small = sem("y_small")
        transposed = sem("transposed")
        xt_hi_done = sem("xt_hi_done")
        xt_lo_done = sem("xt_lo_done")
        win_done = sem("win_done")
        xh_done = sem("xh_done")
        gate_mm_done = sem("gate_mm_done")
        tanh_done = sem("tanh_done")
        inc_done = sem("inc_done")
        turns_done = sem("turns_done")
        round_done = sem("round_done")
        frac_done = sem("frac_done")
        mag_done = sem("mag_done")
        mag2_done = sem("mag2_done")
        z_done = sem("z_done")
        norm_done = sem("norm_done")
        gain_done = sem("gain_done")
        sin_done = sem("sin_done")
        abs_done = sem("abs_done")
        cos_done = sem("cos_done")
        gsin_done = sem("gsin_done")
        gcos_done = sem("gcos_done")
        cross_done = sem("cross_done")
        cross_pool_done = sem("cross_pool_done")
        fwd_mul_done = sem("fwd_mul_done")
        back_cross_done = sem("back_cross_done")
        back_pool_done = sem("back_pool_done")
        fwd_done = sem("fwd_done")
        scan_done = sem("scan_done")
        back_mul_done = sem("back_mul_done")
        h_done = sem("h_done")
        carry_done = sem("carry_done")
        out_done = sem("out_done")
        y_bn_done = sem("y_bn_done")
        y_stats = sem("y_stats")
        y_scaled = sem("y_scaled")
        y_normed = sem("y_normed")
        x1_ready = sem("x1_ready")

        x_rows = d["x"].rearrange("(t g p) d -> t p g d", g=G, p=P)
        x1_rows = d["x1"].rearrange("(t g p) d -> t p g d", g=G, p=P)
        LAST = NT - 1
        POOL_CHUNKS, DVE_CHUNKS = (0, 1), (2, 3)
        SERVED = DVE_CHUNKS + POOL_CHUNKS
        ORDER = (2, 6, 3, 7, 0, 4, 1, 5)
        PROJECT, GATES = range(2)
        LEAD = 6
        RINGED = [(PROJECT, n) for n in ORDER[:LEAD]]
        for k in range(HC - LEAD):
            RINGED += [(GATES, ORDER[k]), (PROJECT, ORDER[k + LEAD])]
        RINGED += [(GATES, n) for n in ORDER[HC - LEAD:]]

        def tile_of(rows, t):
            if isinstance(t, int):
                return rows[t]
            return rows[bass.ds(t, 1)].rearrange("o p g d -> p (o g) d")

        def steps(eng, step):
            step(0)
            with eng.Fori(0, (NT - 2) // 2) as i:
                for u in range(2):
                    step(2 * i + (1 + u))
            step(LAST)

        def first(t):
            return isinstance(t, int) and t == 0

        def last(t):
            return isinstance(t, int) and t == LAST

        block = ctx.enter_context(nc.Block())

        @block.sync
        def _(sp_):
            sp_.dma_start(x_in[:], tile_of(x_rows, 0)).then_inc(xin_loaded, 16)
            sp_.dma_start(h[:].rearrange("p a c t -> p (a c t)"),
                          d["w_in"].rearrange("p k n -> p (k n)")).then_inc(win_loaded, 16)
            for dst, src in ((b_in, "b_in"), (b_gate, "b_gate"), (a_real, "a_real"), (a_imag, "a_imag"),
                             (ident, "ident"), (bout_raw, "b_out"), (low_row, "low_row")):
                sp_.dma_start(dst[:], d[src]).then_inc(consts_loaded, 16)
            sp_.dma_start(wgate[:], d["w_gate"]).then_inc(consts_loaded, 16)
            sp_.dma_start(wout[:], d["w_out"]).then_inc(wout_loaded, 16)
            sp_.dma_start(x_res[:], tile_of(x_rows, 0)).then_inc(xres_loaded, 16)
            sp_.wait_ge(xn_done, G)
            sp_.dma_start(x_in[:], tile_of(x_rows, 1)).then_inc(xin_loaded, 16)

            def step(t):
                if not first(t):
                    sp_.wait_ge(x1_ready, G * t)
                    after_wait(sp_)
                    sp_.dma_start(tile_of(x1_rows, t - 1), x_res[:]).then_inc(x1_stored, 16)
                    sp_.wait_ge(x1_stored, 16 * t)
                    after_wait(sp_)
                    sp_.dma_start(x_res[:], tile_of(x_rows, t)).then_inc(xres_loaded, 16)

            def step_in(t):
                sp_.wait_ge(xn_done, G * (t + 2))
                after_wait(sp_)
                sp_.dma_start(x_in[:], tile_of(x_rows, t + 2)).then_inc(xin_loaded, 16)

            step_in(0)
            with sp_.Fori(0, (NT - 2) // 2 - 1) as i:
                for u in range(2):
                    step_in(2 * i + (1 + u))
                    step(2 * i + (1 + u))
            step_in(NT - 3)
            step(NT - 3)
            step(NT - 2)
            step(LAST)
            sp_.wait_ge(x1_ready, G * NT)
            sp_.dma_start(tile_of(x1_rows, LAST), x_res[:]).then_inc(x1_stored, 16)
            sp_.wait_ge(x1_stored, 16 * NT)

        @block.gpsimd
        def _(pool):
            pool.memset(neg_half[:], -0.5).then_inc(pool_consts, 1)
            pool.wait_ge(pool_consts, 1)

            def scales(mv, sc, small, n, done):
                after_wait(pool)
                pool.tensor_scalar(sc[:, 0], mv[:, :, 1], EPS, 1.0, ALU.add, ALU.mult).then_inc(small, 1)
                pool.tensor_scalar(sc[:, 1], mv[:, :, 0], -1.0, 0.0, ALU.mult, ALU.add).then_inc(small, 1)
                pool.wait_ge(small, n + 2)
                w = sc.shape[-1]
                pool.tensor_tensor(sc[:, 0], sc[:, 0], neg_half[:, 0:w], ALU.pow).then_inc(small, 1)
                pool.wait_ge(small, n + 3)
                pool.tensor_tensor(sc[:, 1], sc[:, 1], sc[:, 0], ALU.mult).then_inc(done, 1)

            def norm_x(t):
                pool.wait_ge(x_stats, G * (t + 1))
                wait(pool, xn_done, G * t)
                scales(x_mv[:], x_sc[:], x_small, 4 * t, x_small)
                pool.wait_ge(x_small, 4 * t + 4)
                wait(pool, transposed, G * t)
                after_wait(pool)
                for j in range(G):
                    pool.tensor_scalar(xn[:, j], x_in[:, j], x_sc[:, 0, j:j + 1], x_sc[:, 1, j:j + 1],
                                       ALU.mult, ALU.add).then_inc(xn_done, 1)

            def norm_y(t):
                for j in range(G):
                    pool.wait_ge(y_stats, G * t + j + 1)
                    scales(y_mv[:, j:j + 1], y_sc[:, :, j:j + 1], y_small, 3 * (G * t + j), y_scaled)

            def both(plane, c):
                return plane[:, c:c + 1, :].to_broadcast([P, 2, T])

            def cross_products(t):
                for c in POOL_CHUNKS:
                    pool.wait_ge(gsin_done, KC * t + c + 1)
                    wait(pool, h_done, 2 * KC * t)
                    pool.tensor_tensor(cross[:, :, c], xh[:, :, c], both(turns, c), ALU.mult).then_inc(
                        cross_pool_done, 1)

            def back_cross_products(t):
                for c in POOL_CHUNKS:
                    pool.wait_ge(scan_done, 2 * (KC * t + c + 1))
                    pool.tensor_tensor(cross[:, :, c], h[:, :, c], both(sin, c), ALU.mult).then_inc(
                        back_pool_done, 1)

            norm_x(0)
            norm_x(1)

            def step(t):
                cross_products(t)
                if not first(t):
                    norm_y(t - 1)
                if not (isinstance(t, int) and t >= NT - 2):
                    norm_x(t + 2)
                back_cross_products(t)

            step(0)
            with pool.Fori(0, (NT - 2) // 2 - 1) as i:
                for u in range(2):
                    step(2 * i + (1 + u))
            step(NT - 3)
            step(NT - 2)
            step(LAST)
            norm_y(LAST)

        @block.tensor
        def _(pe):
            def transposes(t, js):
                for j in js:
                    pe.wait_ge(xn_done, G * t + j + 1)
                    evacuated(t - 1, len(RINGED) - 4 + j)
                    for c in range(KC):
                        mm = pe.transpose(psum[:, j, c * P:(c + 1) * P], xn[:, j, c * P:(c + 1) * P], ident[:])
                    mm.then_inc(transposed, 1)

            def evacuated(t, r):
                kind, n = RINGED[r]
                if kind == PROJECT:
                    wait(pe, xh_done, HC * t + (ORDER.index(n) + 1) if not before_first(t) else 0)
                else:
                    wait(pe, tanh_done, 2 * (HC * t + (ORDER.index(n) + 1)) if not before_first(t) else 0)

            def before_first(t):
                return isinstance(t, int) and t < 0

            def project_and_gates(t):
                for r, (kind, n) in enumerate(RINGED):
                    bank = psum[:, r % 4, :]
                    if r < 4:
                        if r == 0:
                            pe.wait_ge(xt_lo_done, G * (t + 1))
                    else:
                        evacuated(t, r - 4)
                    if kind == PROJECT:
                        for kc in range(KC):
                            w_hi = win_hi[:, kc, n * P:(n + 1) * P]
                            w_lo = win_lo[:, kc, n * P:(n + 1) * P]
                            pe.matmul(bank, w_hi, xt_hi[:, kc], start=(kc == 0), stop=False)
                            pe.matmul(bank, w_hi, xt_lo[:, kc], start=False, stop=False)
                            mm = pe.matmul(bank, w_lo, xt_hi[:, kc], start=False, stop=(kc == KC - 1))
                        mm.then_inc(win_done, 1)
                    else:
                        pe.wait_ge(xh_done, HC * t + (ORDER.index(n) + 1))
                        pe.matmul(bank, wgate[:, n], xh[:, n // KC, n % KC],
                                  start=True, stop=True).then_inc(gate_mm_done, 1)

            def out_project(t, js=range(G)):
                for j in js:
                    if j == 0:
                        pe.wait_ge(h_done, 2 * KC * (t + 1))
                    bank = psum[:, OUT0 + j, :]
                    pe.matmul(bank, ones_row[:], bout[:], start=True, stop=False)
                    for k in range(HC):
                        mm = pe.matmul(bank, h[:, k // KC, k % KC, j * P:(j + 1) * P], wout[:, k],
                                       start=False, stop=(k == HC - 1))
                    mm.then_inc(out_done, 1)

            pe.wait_ge(consts_loaded, 16 * 8)
            transposes(0, range(G))
            pe.wait_ge(win_hi_done, KC)
            pe.wait_ge(win_lo_done, KC)
            project_and_gates(0)

            def step(t):
                if not last(t):
                    transposes(t + 1, (0, 1, 2))
                if not first(t):
                    out_project(t - 1, (0,))
                if not last(t):
                    transposes(t + 1, (3,))
                if not first(t):
                    out_project(t - 1, (1, 2, 3))
                if not last(t):
                    project_and_gates(t + 1)
                if first(t):
                    pe.wait_ge(wout_loaded, 16)
                    pe.wait_ge(dve_consts, 4)

            steps(pe, step)
            out_project(LAST)

        @block.scalar
        def _(act):
            act.wait_ge(win_loaded, 16)
            hw = h[:].rearrange("p a c t -> p (a c t)").rearrange("p (k n) -> p k n", k=KC)
            for kc in range(KC):
                act.activation(win_hi[:, kc], hw[:, kc], ACT.Copy).then_inc(win_hi_done, 1)
            act.wait_ge(consts_loaded, 16 * 8)
            act.activation(sp[:, 0], a_real[:], ACT.Abs).then_inc(act_small, 1)
            act.activation(bout_hi[:], bout_raw[:], ACT.Copy).then_inc(act_small, 1)
            act.wait_ge(act_small, 2)
            act.activation(sp[:, 1], sp[:, 0], ACT.Exp, scale=-1.0).then_inc(act_small, 1)

            def xt_high(t, js):
                for j in js:
                    act.wait_ge(transposed, G * t + j + 1)
                    if j == 0:
                        wait(act, win_done, HC * t)
                    act.activation(xt_hi[:, :, j * P:(j + 1) * P],
                                   psum[:, j, :].rearrange("p (c q) -> p c q", c=KC),
                                   ACT.Copy).then_inc(xt_hi_done, 1)

            def evacuate(t, part):
                for r, (kind, n) in list(enumerate(RINGED))[part]:
                    bank = psum[:, r % 4, :]
                    k = ORDER.index(n)
                    if kind == PROJECT:
                        act.wait_ge(win_done, HC * t + k + 1)
                        wait(act, fwd_done, 2 * (KC * (t - 1) + SERVED.index(n % KC) + 1))
                        act.activation(xh[:, n // KC, n % KC], bank, ACT.Identity,
                                       bias=b_in[:, n:n + 1]).then_inc(xh_done, 1)
                        continue
                    act.wait_ge(gate_mm_done, HC * t + k + 1)
                    if k == 0:
                        wait(act, gain_done, KC * t)
                        wait(act, mag_done, KC * t)
                        wait(act, inc_done, KC * t)
                    to = slice(64 * (n % 2), 64 * (n % 2) + 64)
                    act.activation(tanh_x[to, n // 2], bank[0:64], ACT.Tanh,
                                   bias=b_gate[0:64, n:n + 1], scale=0.5).then_inc(tanh_done, 1)
                    act.activation(tanh_a[to, n // 2], bank[64:128], ACT.Tanh,
                                   bias=b_gate[64:128, n:n + 1], scale=0.5).then_inc(tanh_done, 1)

            def exps(t):
                act.wait_ge(tanh_done, 2 * HC * (t + 1))
                for c in range(KC):
                    wait(act, gcos_done, KC * t)
                    act.activation(gain[:, c], tanh_a[:, c], ACT.Exp, bias=mag2_k[:, c:c + 1],
                                   scale=mag2_k[:, c:c + 1]).then_inc(mag2_done, 1)
                for c in range(KC):
                    wait(act, scan_done, 2 * (KC * (t - 1) + c + 1))
                    act.activation(mag[:, c], tanh_a[:, c], ACT.Exp, bias=mag_k[:, c:c + 1],
                                   scale=mag_k[:, c:c + 1]).then_inc(mag_done, 1)

            def norm_roots(t):
                for c in range(KC):
                    act.wait_ge(z_done, KC * t + c + 1)
                    act.activation(gain[:, c], gain[:, c], ACT.Sqrt, scale=-0.25).then_inc(norm_done, 1)

            def sines(t):
                for c in range(KC):
                    act.wait_ge(frac_done, KC * t + c + 1)
                    wait(act, back_mul_done, KC * t)
                    act.activation(sin[:, c], frac[:, c], ACT.Sin, scale=-TWO_PI_SAFE).then_inc(sin_done, 1)
                for c in range(KC):
                    act.activation(cos[:, c], frac[:, c], ACT.Abs).then_inc(abs_done, 1)
                for c in range(KC):
                    act.wait_ge(abs_done, KC * t + c + 1)
                    act.activation(cos[:, c], cos[:, c], ACT.Sin, bias=halfpi[:, 0:1],
                                   scale=-TWO_PI_SAFE).then_inc(cos_done, 1)

            def y_normalise(t):
                for j in range(G):
                    act.wait_ge(y_scaled, G * t + j + 1)
                    act.activation(psum[:, OUT0 + j, :], psum[:, OUT0 + j, :], ACT.Identity,
                                   bias=y_sc[:, 1, j:j + 1], scale=y_sc[:, 0, j:j + 1]).then_inc(y_normed, 1)

            xt_high(0, range(G))
            act.wait_ge(dve_consts, 4)
            evacuate(0, slice(None))

            def step(t):
                if not last(t):
                    xt_high(t + 1, (0, 1, 2))
                exps(t)
                if not last(t):
                    xt_high(t + 1, (3,))
                norm_roots(t)
                sines(t)
                if not last(t):
                    evacuate(t + 1, slice(0, 1))
                if not first(t):
                    y_normalise(t - 1)
                if not last(t):
                    evacuate(t + 1, slice(1, None))

            steps(act, step)
            y_normalise(LAST)

        @block.vector
        def _(dve):
            def x_statistics(t):
                dve.wait_ge(xin_loaded, 16 * (t + 1))
                wait(dve, x_stats, G * t)
                wait(dve, xn_done, G * t)
                for j in range(G):
                    dve.bn_stats(x_bn[:, j], x_in[:, j]).then_inc(x_bn_done, 1)
                for j in range(G):
                    dve.wait_ge(x_bn_done, G * t + j + 1)
                    after_wait(dve)
                    dve.bn_aggr(x_mv[:, j], x_bn[:, j]).then_inc(x_stats, 1)

            def xt_low(t, js):
                for j in js:
                    dve.wait_ge(xt_hi_done, G * t + j + 1)
                    at = slice(j * P, (j + 1) * P)
                    dve.tensor_tensor(xt_lo[:, :, at], psum[:, j, :].rearrange("p (c q) -> p c q", c=KC),
                                      xt_hi[:, :, at].bitcast(F32), ALU.subtract).then_inc(xt_lo_done, 1)

            dve.memset(ones[:], 1.0).then_inc(dve_consts, 1)
            dve.memset(halfpi[:], math.pi / 2).then_inc(dve_consts, 1)
            dve.memset(carry[:], 0.0).then_inc(carry_done, 1)
            dve.memset(keep[:], 1.0).then_inc(dve_small, 1)
            dve.wait_ge(dve_small, 1)
            dve.memset(keep[:, 0:NT + 1:TPB], 0.0).then_inc(dve_small, 1)
            x_statistics(0)
            dve.wait_ge(dve_consts, 1)
            dve.tensor_copy(ones_row[:], ones[0:2, 0:P]).then_inc(dve_consts, 1)
            hw = h[:].rearrange("p a c t -> p (a c t)").rearrange("p (k n) -> p k n", k=KC)
            for kc in range(KC):
                dve.wait_ge(win_hi_done, kc + 1)
                dve.tensor_tensor(win_lo[:, kc], hw[:, kc], win_hi[:, kc].bitcast(F32),
                                  ALU.subtract).then_inc(win_lo_done, 1)
            small = [2]

            def link(ins):
                small[0] += 1
                ins.then_inc(dve_small, 1)
                dve.wait_ge(dve_small, small[0])

            dve.wait_ge(act_small, 3)
            link(dve.scalar_tensor_tensor(bout[:], bout_hi[:].bitcast(F32), low_row[:, 0:1], bout_raw[:],
                                          ALU.mult, ALU.add))
            link(dve.tensor_scalar(b_gate[:], b_gate[:], 0.5, None, ALU.mult))
            link(dve.tensor_scalar(half_turn[:], a_imag[:], 1 / (4 * math.pi), None, ALU.mult))
            link(dve.tensor_scalar(sp[:, 2], sp[:, 1], 2.0, None, ALU.add))
            link(dve.reciprocal(sp[:, 3], sp[:, 2]))
            link(dve.tensor_tensor(sp[:, 3], sp[:, 3], sp[:, 1], ALU.mult))
            link(dve.tensor_tensor(sp[:, 4], sp[:, 3], sp[:, 3], ALU.mult))
            link(dve.tensor_scalar(sp[:, 5], sp[:, 4], 1 / 17, 1 / 15, ALU.mult, ALU.add))
            for k in (13, 11, 9, 7, 5, 3, 1):
                link(dve.tensor_tensor(sp[:, 5], sp[:, 5], sp[:, 4], ALU.mult))
                link(dve.tensor_scalar(sp[:, 5], sp[:, 5], 1 / k, None, ALU.add))
            link(dve.tensor_tensor(sp[:, 5], sp[:, 5], sp[:, 3], ALU.mult))
            link(dve.tensor_scalar(sp[:, 2], a_real[:], 0.0, 0.5, ALU.max, ALU.mult))
            link(dve.tensor_tensor(sp[:, 5], sp[:, 5], sp[:, 2], ALU.add))
            link(dve.tensor_scalar(mag_k[:], sp[:, 5], LOG_A_SCALE, None, ALU.mult))
            dve.tensor_scalar(mag2_k[:], sp[:, 5], 2 * LOG_A_SCALE, None, ALU.mult).then_inc(dve_consts, 1)
            x_statistics(1)
            xt_low(0, range(G))

            def turn_sums(t):
                dve.wait_ge(tanh_done, 2 * HC * (t + 1))
                for c in range(KC):
                    wait(dve, fwd_mul_done, KC * t)
                    dve.tensor_scalar(turns[:, c], tanh_a[:, c], half_turn[:, c:c + 1], half_turn[:, c:c + 1],
                                      ALU.mult, ALU.add).then_inc(inc_done, 1)
                for c in range(KC):
                    dve.wait_ge(inc_done, KC * t + c + 1)
                    dve.tensor_tensor_scan(turns[:, c], ones[:], turns[:, c], 0.0,
                                           ALU.mult, ALU.add).then_inc(turns_done, 1)

            def fractions(t):
                for c in range(KC):
                    dve.wait_ge(turns_done, KC * t + c + 1)
                    dve.tensor_scalar(frac[:, c], turns[:, c], MAGIC, None, ALU.add).then_inc(round_done, 1)
                for c in range(KC):
                    dve.wait_ge(round_done, KC * t + c + 1)
                    dve.scalar_tensor_tensor(frac[:, c], frac[:, c], MAGIC, turns[:, c],
                                             ALU.subtract, ALU.subtract).then_inc(frac_done, 1)

            def norms(t):
                for c in range(KC):
                    dve.wait_ge(mag2_done, KC * t + c + 1)
                    dve.tensor_scalar(gain[:, c], gain[:, c], 1.0, -1e-6, ALU.subtract,
                                      ALU.min).then_inc(z_done, 1)

            def gains(t):
                for c in range(KC):
                    dve.wait_ge(norm_done, KC * t + c + 1)
                    dve.scalar_tensor_tensor(gain[:, c], tanh_x[:, c], 1.0, gain[:, c],
                                             ALU.add, ALU.mult).then_inc(gain_done, 1)
                for c in range(KC):
                    dve.wait_ge(gain_done, KC * t + c + 1)
                    dve.wait_ge(sin_done, KC * t + c + 1)
                    dve.tensor_tensor(turns[:, c], gain[:, c], sin[:, c], ALU.mult).then_inc(gsin_done, 1)

            def both(plane, c):
                return plane[:, c:c + 1, :].to_broadcast([P, 2, T])

            def rotate_products(t):
                for n, c in enumerate(DVE_CHUNKS):
                    dve.wait_ge(gsin_done, KC * (t + 1))
                    wait(dve, h_done, 2 * KC * t)
                    dve.tensor_tensor(cross[:, :, c], xh[:, :, c], both(turns, c), ALU.mult).then_inc(cross_done, 1)
                for c in range(KC):
                    dve.wait_ge(cos_done, KC * t + c + 1)
                    dve.tensor_tensor(frac[:, c], gain[:, c], cos[:, c], ALU.mult).then_inc(gcos_done, 1)
                for n, c in enumerate(SERVED):
                    if c in DVE_CHUNKS:
                        dve.wait_ge(cross_done, len(DVE_CHUNKS) * t + n + 1)
                    else:
                        dve.wait_ge(cross_pool_done, len(POOL_CHUNKS) * t + n - len(DVE_CHUNKS) + 1)
                    dve.wait_ge(gcos_done, KC * t + c + 1)
                    dve.tensor_tensor(xh[:, :, c], xh[:, :, c], both(frac, c), ALU.mult).then_inc(fwd_mul_done, 1)

                for c in SERVED:
                    dve.wait_ge(fwd_mul_done, KC * t + SERVED.index(c) + 1)
                    dve.tensor_tensor(cross[:, 1, c], xh[:, 0, c], cross[:, 1, c], ALU.add).then_inc(fwd_done, 1)
                    dve.tensor_tensor(cross[:, 0, c], xh[:, 1, c], cross[:, 0, c],
                                      ALU.subtract).then_inc(fwd_done, 1)

            def recur(t):
                wait(dve, out_done, G * t)
                if first(t):
                    dve.wait_ge(win_lo_done, KC)
                dve.wait_ge(carry_done, t + 1)
                dve.wait_ge(mag_done, KC * (t + 1))
                for c in range(KC):
                    for ri in range(2):
                        dve.wait_ge(fwd_done, 2 * (KC * t + SERVED.index(c)) + ri + 1)
                        dve.tensor_tensor_scan(h[:, ri, c], mag[:, c], cross[:, 1 - ri, c], carry[:, ri, c:c + 1],
                                               ALU.mult, ALU.add).then_inc(scan_done, 1)
                for n, c in enumerate(DVE_CHUNKS):
                    dve.wait_ge(scan_done, 2 * (KC * t + c + 1))
                    dve.tensor_tensor(cross[:, :, c], h[:, :, c], both(sin, c), ALU.mult).then_inc(back_cross_done, 1)
                for n, c in enumerate(SERVED):
                    if c in DVE_CHUNKS:
                        dve.wait_ge(back_cross_done, len(DVE_CHUNKS) * t + n + 1)
                    else:
                        dve.wait_ge(back_pool_done, len(POOL_CHUNKS) * t + n - len(DVE_CHUNKS) + 1)
                    dve.tensor_tensor(h[:, :, c], h[:, :, c], both(cos, c), ALU.mult).then_inc(back_mul_done, 1)
                for n, c in enumerate(SERVED):
                    dve.wait_ge(back_mul_done, KC * t + n + 1)
                    dve.tensor_tensor(h[:, 0, c], h[:, 0, c], cross[:, 1, c], ALU.subtract).then_inc(h_done, 1)
                    dve.tensor_tensor(h[:, 1, c], h[:, 1, c], cross[:, 0, c], ALU.add).then_inc(h_done, 1)
                dve.wait_ge(h_done, 2 * KC * (t + 1))
                at = slice(t + 1, t + 2) if isinstance(t, int) else bass.ds(t + 1, 1)
                dve.tensor_scalar(carry[:], h[:, :, :, T - 1], keep[:, at], None, ALU.mult).then_inc(carry_done, 1)

            def y_stat(t, j):
                dve.wait_ge(out_done, G * t + j + 1)
                dve.bn_stats(y_bn[:, j], psum[:, OUT0 + j, :]).then_inc(y_bn_done, 1)

            def y_stat_sum(t, j):
                dve.wait_ge(y_bn_done, G * t + j + 1)
                after_wait(dve)
                dve.bn_aggr(y_mv[:, j], y_bn[:, j]).then_inc(y_stats, 1)

            def y_add(t, j):
                dve.wait_ge(y_normed, G * t + j + 1)
                dve.wait_ge(xres_loaded, 16 * (t + 1))
                dve.tensor_tensor(x_res[:, j], psum[:, OUT0 + j, :], x_res[:, j], ALU.add).then_inc(x1_ready, 1)

            def y_statistics(t):
                for j in range(G):
                    y_stat(t, j)
                    if j > 0:
                        y_stat_sum(t, j - 1)
                y_stat_sum(t, G - 1)

            def step(t):
                if not last(t):
                    xt_low(t + 1, (0, 1, 2))
                turn_sums(t)
                norms(t)
                fractions(t)
                if not last(t):
                    xt_low(t + 1, (3,))
                gains(t)
                rotate_products(t)
                if not first(t):
                    y_statistics(t - 1)
                if not (isinstance(t, int) and t >= NT - 2):
                    x_statistics(t + 2)
                if not first(t):
                    for j in range(G):
                        y_add(t - 1, j)
                recur(t)

            step(0)
            with dve.Fori(0, (NT - 2) // 2 - 1) as i:
                for u in range(2):
                    step(2 * i + (1 + u))
            step(NT - 3)
            step(NT - 2)
            step(LAST)
            y_statistics(LAST)
            for j in range(G):
                y_add(LAST, j)


def phase_b(nc, d, NQ=NE):
    with ExitStack() as ctx:
        def sb(name, shape, dt=F32):
            return ctx.enter_context(nc.sbuf_tensor(name, shape, dt))

        def sem(name):
            return ctx.enter_context(nc.semaphore(name))

        sw1_hi, sw1_lo = sb("sw1_hi", [P, KC, HS], F32R), sb("sw1_lo", [P, KC, HS], F32R)
        sw3_hi, sw3_lo = sb("sw3_hi", [P, KC, HS], F32R), sb("sw3_lo", [P, KC, HS], F32R)
        sw2_hi, sw2_lo = sb("sw2_hi", [P, HS // P, D], F32R), sb("sw2_lo", [P, HS // P, D], F32R)
        w1_hi, w1_lo = sb("w1_hi", [P, 2, KC, HR], F32R), sb("w1_lo", [P, 2, KC, HR], F32R)
        w2_hi, w2_lo = sb("w2_hi", [P, 2, KC, D], F32R), sb("w2_lo", [P, 2, KC, D], F32R)
        stage = sb("stage", [P, RING, D])
        xt_hi, xt_lo = sb("fx_hi", [P, KC, T], F32R), sb("fx_lo", [P, KC, T], F32R)
        x1 = sb("x1_tile", [P, 2, G, D])
        xn = sb("fxn", [P, 2, D])
        gate = sb("gate", [P, T])
        hid_hi, hid_lo = sb("hid_hi", [P, 2, T], F32R), sb("hid_lo", [P, 2, T], F32R)
        brow_raw = sb("brow_raw", [6, D])
        brow_hi = sb("brow_hi", [6, D], F32R)
        brow = sb("brow", [6, D], F32R)
        bsel_raw = sb("bsel_raw", [6, P])
        bsel = sb("bsel", [6, P], F32R)
        low_rows = sb("low_rows", [6, 1])
        ident = sb("f_ident", [P, P])
        b_s1, b_s3 = sb("b_s1", [P, HS // P]), sb("b_s3", [P, HS // P])
        b_r1 = sb("b_r1", [P, (NE + 1) * KC])
        neg_half = sb("f_neg_half", [P, G])
        x_bn, x_mv, x_sc = sb("fx_bn", [P, G, 6]), sb("fx_mv", [P, G, 2]), sb("fx_sc", [P, 2, G])
        y_bn, y_mv, y_sc = sb("fy_bn", [P, G, 6]), sb("fy_mv", [P, G, 2]), sb("fy_sc", [P, 2, G])
        psum = ctx.enter_context(nc.psum_tensor("psum_b", [P, 8, 512], F32))
        HID0, OUT0 = 2, 4

        consts_loaded = sem("f_consts_loaded")
        pool_consts = sem("f_pool_consts")
        x1_loaded = [sem(f"f_x1_loaded{k}") for k in range(2)]
        x2_stored = [sem(f"f_x2_stored{k}") for k in range(2)]
        piece_loaded = [sem(f"f_piece_loaded{k}") for k in range(RING)]
        brow_loaded = sem("f_brow_loaded")
        bsel_done = sem("f_bsel_done")
        brow_hi_done = sem("f_brow_hi_done")
        brow_done = sem("f_brow_done")
        piece_hi_done = sem("f_piece_hi_done")
        piece_lo_done = sem("f_piece_lo_done")
        x_bn_done = sem("f_x_bn_done")
        x_stats = sem("f_x_stats")
        x_small = sem("f_x_small")
        xn_done = sem("f_xn_done")
        transposed = sem("f_transposed")
        xt_hi_done = sem("f_xt_hi_done")
        xt_lo_done = sem("f_xt_lo_done")
        hid_mm_done = sem("f_hid_mm_done")
        act_done = sem("f_act_done")
        prod_done = sem("f_prod_done")
        hid_hi_done = sem("f_hid_hi_done")
        hid_lo_done = sem("f_hid_lo_done")
        out_unit_done = sem("f_out_unit_done")
        out_done = sem("f_out_done")
        y_bn_done = sem("f_y_bn_done")
        y_stats = sem("f_y_stats")
        y_small = sem("f_y_small")
        y_scaled = sem("f_y_scaled")
        y_normed = sem("f_y_normed")
        x2_ready = sem("f_x2_ready")

        OLD, SHARED, NEW = range(3)
        kinds = [OLD] * KC + [SHARED] * (HS // P) + [NEW] * KC
        UN = len(kinds)
        starts = [sum(2 if x == SHARED else 1 for x in kinds[:k]) for k in range(UN + 1)]
        HM = starts[UN]

        by_class = "(g p r) d -> r p g d"
        x1_rows = d["x1"].rearrange(by_class, p=P, r=NE)
        out_rows = d["out"].rearrange(by_class, p=P, r=NE)

        def rows_of(rows, q, hf):
            at = slice(hf * G, (hf + 1) * G)
            if isinstance(q, int):
                return rows[5 * q % NE, :, at]
            return rows[bass.ds(5 * q % NE, 1), :, at].rearrange("o p g d -> p (o g) d")

        def steps(eng, step):
            for hf in range(2):
                step(hf, 0, hf, 0)
            if NQ > 2:
                with eng.Fori(0, (NQ - 2) // 2) as i:
                    for v in range(2):
                        for hf in range(2):
                            q = 2 * i + (1 + v)
                            step(4 * i + (2 * (1 + v) + hf), q, hf, (1 + v) % 2)
            for hf in range(2):
                step(2 * (NQ - 1) + hf, NQ - 1, hf, (NQ - 1) % 2)

        def is_last(m):
            return isinstance(m, int) and m == 2 * NQ - 1

        def first(m):
            return isinstance(m, int) and m == 0

        def expert_pieces(slot):
            return ([(w1_hi[:, slot, k], w1_lo[:, slot, k], 1.0) for k in range(KC)]
                    + [(w2_hi[:, slot, k], w2_lo[:, slot, k], 0.5) for k in range(KC)])

        def shared_pieces(half):
            at = slice(half * 512, (half + 1) * 512)
            return ([(sw1_hi[:, k, at], sw1_lo[:, k, at], 1.0) for k in range(KC)]
                    + [(sw3_hi[:, k, at], sw3_lo[:, k, at], 1.0) for k in range(KC)]
                    + [(sw2_hi[:, k], sw2_lo[:, k], 1.0) for k in range(half * KC, half * KC + KC)])

        FIRST = expert_pieces(0) + shared_pieces(0) + shared_pieces(1) + expert_pieces(1)
        NF = len(FIRST)

        def pieces_after(m, q, hf, par, k):
            if first(m):
                cuts = [0, 8, 11, 14, 17, 20, 23, 26, 29, 32, 34, 36, 38, 40, 40, 40, 40, 40]
                return [(n, FIRST[n]) for n in range(cuts[k + 1], cuts[k + 2])]
            more = not (isinstance(q, int) and q == NQ - 1)
            if hf == 1 and more and 5 <= k < 5 + 8:
                return [(8 * q + (NF + k - 5), expert_pieces(par)[k - 5])]
            return []

        block = ctx.enter_context(nc.Block())

        @block.sync
        def _(sp):
            def load_piece(n, slot, src):
                sp.dma_start(stage[:, slot], src).then_inc(piece_loaded[slot], 16)

            w1d = d["w1"].rearrange("e (k p) n -> e k p n", p=P)
            w2d = d["w2"].rearrange("e (k p) n -> e k p n", p=P)

            def of_expert(j, k):
                src, kk = (w1d, k) if k < KC else (w2d, k - KC)
                if isinstance(j, int):
                    return src[(NE - 1) * j % NE, kk]
                return src[bass.ds((NE - 1) * j % NE, 1), kk].rearrange("e p n -> p (e n)")

            def of_shared(half, k):
                if k < 2 * KC:
                    w = d["sw1"] if k < KC else d["sw3"]
                    return w.rearrange("(k p) n -> k p n", p=P)[k % KC, :, half * 512:(half + 1) * 512]
                return d["sw2"].rearrange("(k p) n -> k p n", p=P)[half * KC + k - 2 * KC]

            sources = ([of_expert(0, k) for k in range(8)] + [of_shared(0, k) for k in range(12)]
                       + [of_shared(1, k) for k in range(12)] + [of_expert(1, k) for k in range(8)])
            sp.dma_start(x1[:, 0], rows_of(x1_rows, 0, 0)).then_inc(x1_loaded[0], 16)
            for dst, src in ((ident, "ident"), (bsel_raw, "bsel"), (low_rows, "low_rows"), (b_s1, "b_s1"), (b_s3, "b_s3"), (b_r1, "b_r1")):
                sp.dma_start(dst[:], d[src]).then_inc(consts_loaded, 16)
            for at in (0, 3):
                sp.dma_start(brow_raw[at:at + 1, :], d["b_s2"]).then_inc(consts_loaded, 16)
                sp.dma_start(brow_raw[at + 1:at + 3, :], d["b_r2"][0:2]).then_inc(brow_loaded, 16)
            for n in range(NF):
                wait(sp, piece_lo_done, n - RING + 1)
                load_piece(n, n % RING, sources[n])
                if n == 7:
                    sp.dma_start(x1[:, 1], rows_of(x1_rows, 0, 1)).then_inc(x1_loaded[1], 16)

            def step(m, q, hf, par):
                if not first(m):
                    sp.wait_ge(x2_ready, G * m)
                    after_wait(sp)
                    prev_q, prev_hf = (q, 0) if hf == 1 else (q - 1, 1)
                    sp.dma_start(rows_of(out_rows, prev_q, prev_hf), x1[:, 1 - hf]).then_inc(x2_stored[1 - hf], 16)
                    if not is_last(m):
                        n_stored = q + 1 if hf == 1 else q
                        sp.wait_ge(x2_stored[1 - hf], 16 * n_stored)
                        after_wait(sp)
                        next_q, next_hf = (q + 1, 0) if hf == 1 else (q, 1)
                        sp.dma_start(x1[:, next_hf], rows_of(x1_rows, next_q, next_hf)).then_inc(
                            x1_loaded[next_hf], 16)
                if hf == 0 and not (isinstance(q, int) and q == NQ - 1):
                    sp.wait_ge(brow_done, q + 1)
                    after_wait(sp)
                    rows = d["b_r2"][q + 1:q + 3] if isinstance(q, int) else d["b_r2"][bass.ds(q + 1, 2)]
                    for at in (0, 3):
                        sp.dma_start(brow_raw[at + 1:at + 3, :], rows).then_inc(brow_loaded, 16)
                if hf == 1 and not (isinstance(q, int) and q == NQ - 1):
                    for k in range(8):
                        sp.wait_ge(piece_lo_done, 8 * q + (NF + k - RING + 1))
                        after_wait(sp)
                        load_piece(None, k % RING, of_expert(q + 2, k))

            steps(sp, step)
            sp.wait_ge(x2_ready, G * 2 * NQ)
            sp.dma_start(rows_of(out_rows, NQ - 1, 1), x1[:, 1]).then_inc(x2_stored[1], 16)
            for k in range(2):
                sp.wait_ge(x2_stored[k], 16 * NQ)

        @block.gpsimd
        def _(pool):
            pool.memset(neg_half[:], -0.5).then_inc(pool_consts, 1)
            pool.wait_ge(pool_consts, 1)

            def scales(mv, sc, small, n, done, eps):
                after_wait(pool)
                pool.tensor_scalar(sc[:, 0], mv[:, :, 1], eps, 1.0, ALU.add, ALU.mult).then_inc(small, 1)
                pool.tensor_scalar(sc[:, 1], mv[:, :, 0], -1.0, 0.0, ALU.mult, ALU.add).then_inc(small, 1)
                pool.wait_ge(small, n + 2)
                w = sc.shape[-1]
                pool.tensor_tensor(sc[:, 0], sc[:, 0], neg_half[:, 0:w], ALU.pow).then_inc(small, 1)
                pool.wait_ge(small, n + 3)
                pool.tensor_tensor(sc[:, 1], sc[:, 1], sc[:, 0], ALU.mult).then_inc(done, 1)

            def norm_x(m, hf):
                pool.wait_ge(x_stats, G * (m + 1))
                wait(pool, xn_done, G * m)
                scales(x_mv[:], x_sc[:], x_small, 4 * m, x_small, EPS)
                pool.wait_ge(x_small, 4 * m + 4)
                for j in range(G):
                    wait(pool, transposed, G * m + j - 1)
                    after_wait(pool)
                    pool.tensor_scalar(xn[:, j % 2], x1[:, hf, j], x_sc[:, 0, j:j + 1], x_sc[:, 1, j:j + 1],
                                       ALU.mult, ALU.add).then_inc(xn_done, 1)

            def norm_y(m):
                for j in range(G):
                    pool.wait_ge(y_stats, G * m + j + 1)
                    scales(y_mv[:, j:j + 1], y_sc[:, :, j:j + 1], y_small, 3 * (G * m + j), y_scaled, 4 * EPS)

            norm_x(0, 0)

            def step(m, q, hf, par):
                if not first(m):
                    norm_y(m - 1)
                if not is_last(m):
                    norm_x(m + 1, 1 - hf)

            steps(pool, step)
            norm_y(2 * NQ - 1)

        @block.tensor
        def _(pe):
            def transposes(m, js):
                for j in js:
                    pe.wait_ge(xn_done, G * m + j + 1)
                    wait(pe, xt_lo_done, G * m + j - 1)
                    for c in range(KC):
                        mm = pe.transpose(psum[:, j % 2, c * P:(c + 1) * P], xn[:, j % 2, c * P:(c + 1) * P],
                                          ident[:])
                    mm.then_inc(transposed, 1)

            def split_product(bank, w_hi, w_lo, at):
                for kc in range(KC):
                    pe.matmul(bank, w_hi[:, kc, at], xt_hi[:, kc], start=(kc == 0), stop=False)
                    pe.matmul(bank, w_hi[:, kc, at], xt_lo[:, kc], start=False, stop=False)
                    mm = pe.matmul(bank, w_lo[:, kc, at], xt_hi[:, kc], start=False, stop=(kc == KC - 1))
                mm.then_inc(hid_mm_done, 1)

            def hidden(m, par, k):
                kind = kinds[k]
                if kind == SHARED:
                    at = slice((k - KC) * P, (k - KC + 1) * P)
                    if k == KC:
                        pe.wait_ge(hid_lo_done, UN * m + k - 1)
                    else:
                        pe.wait_ge(act_done, UN * m + k)
                    split_product(psum[:, HID0, :], sw1_hi, sw1_lo, at)
                    pe.wait_ge(hid_lo_done, UN * m + k)
                    split_product(psum[:, HID0 + 1, :], sw3_hi, sw3_lo, at)
                    return
                c = k if kind == OLD else k - (UN - KC)
                slot = par if kind == OLD else 1 - par
                if kind == NEW and c == 0:
                    pe.wait_ge(act_done, UN * m + k)
                elif kind == NEW and c == 1:
                    pe.wait_ge(hid_lo_done, UN * m + k - 1)
                else:
                    wait(pe, hid_lo_done, UN * m + k - 1)
                split_product(psum[:, HID0 + c % 2, :], w1_hi[:, slot], w1_lo[:, slot],
                              slice(c * P, (c + 1) * P))

            def output(m, q, par, k, js=range(G)):
                kind = kinds[k]
                if kind == SHARED:
                    w_hi, w_lo = sw2_hi[:, k - KC], sw2_lo[:, k - KC]
                else:
                    c = k if kind == OLD else k - (UN - KC)
                    slot = par if kind == OLD else 1 - par
                    w_hi, w_lo = w2_hi[:, slot, c], w2_lo[:, slot, c]
                pe.wait_ge(hid_lo_done, UN * m + k + 1)
                for j in js:
                    at = slice(j * P, (j + 1) * P)
                    bank = psum[:, OUT0 + j, :]
                    if k == 0:
                        wait(pe, x2_ready, G * (m - 1) + j + 1)
                        if j == 0:
                            pe.wait_ge(brow_done, q + 1)
                        pe.matmul(bank, bsel[:], brow[:], start=True, stop=False)
                    pe.matmul(bank, hid_hi[:, k % 2, at], w_hi, start=False, stop=False)
                    pe.matmul(bank, hid_hi[:, k % 2, at], w_lo, start=False, stop=False)
                    mm = pe.matmul(bank, hid_lo[:, k % 2, at], w_hi, start=False, stop=(k == UN - 1))
                    if k == UN - 1:
                        mm.then_inc(out_done, 1)
                    elif j == G - 1:
                        mm.then_inc(out_unit_done, 1)

            pe.wait_ge(consts_loaded, 16 * 8)
            pe.wait_ge(bsel_done, 1)
            transposes(0, range(G))

            def step(m, q, hf, par):
                pe.wait_ge(xt_lo_done, G * (m + 1))
                for k in range(UN):
                    if first(m) and k in (0, 4, 8, 12):
                        pe.wait_ge(piece_lo_done, {0: 8, 4: 20, 8: 32, 12: 40}[k])
                    elif k == UN - KC and hf == 0 and not first(m):
                        pe.wait_ge(piece_lo_done, 8 * q + NF)
                    if k == UN - 1 and not is_last(m):
                        transposes(m + 1, (0, 1))
                    hidden(m, par, k)
                    if k > 0:
                        output(m, q, par, k - 1)
                output(m, q, par, UN - 1, (0, 1))
                if not is_last(m):
                    transposes(m + 1, (2,))
                output(m, q, par, UN - 1, (2,))
                if not is_last(m):
                    transposes(m + 1, (3,))
                output(m, q, par, UN - 1, (3,))

            steps(pe, step)

        @block.scalar
        def _(act):
            def xt_high(m, js):
                for j in js:
                    act.wait_ge(transposed, G * m + j + 1)
                    if j == 0:
                        wait(act, hid_mm_done, HM * m)
                    act.activation(xt_hi[:, :, j * P:(j + 1) * P],
                                   psum[:, j % 2, :].rearrange("p (c q) -> p c q", c=KC),
                                   ACT.Copy).then_inc(xt_hi_done, 1)

            def pieces_high(m, q, hf, par, k):
                for n, (w_hi, _, scale) in pieces_after(m, q, hf, par, k):
                    slot = n % RING if isinstance(n, int) else (k - 5) % RING
                    turn = n // RING if isinstance(n, int) else 2 * q + (NF + k - 5) // RING
                    act.wait_ge(piece_loaded[slot], 16 * (turn + 1))
                    if not first(m):
                        act.wait_ge(out_unit_done, (UN - 1) * m + KC)
                    act.activation(w_hi, stage[:, slot], ACT.Copy, scale=scale).then_inc(piece_hi_done, 1)

            def activate(m, q, k):
                kind = kinds[k]
                act.wait_ge(hid_mm_done, HM * m + starts[k] + 1)
                if kind == SHARED:
                    wait(act, prod_done, (HS // P) * m + k - KC)
                    act.activation(gate[:], psum[:, HID0, :], ACT.Silu,
                                   bias=b_s1[:, k - KC:k - KC + 1]).then_inc(act_done, 1)
                else:
                    c = k if kind == OLD else k - (UN - KC)
                    j = q if kind == OLD else q + 1
                    col = KC * j + c
                    at = slice(col, col + 1) if isinstance(col, int) else bass.ds(col, 1)
                    bank = psum[:, HID0 + c % 2, :]
                    after_wait(act)
                    act.activation(bank, bank, ACT.Gelu, bias=b_r1[:, at]).then_inc(act_done, 1)

            def hidden_high(m, k):
                kind = kinds[k]
                if kind == SHARED:
                    act.wait_ge(prod_done, (HS // P) * m + k - KC + 1)
                    bank = psum[:, HID0 + 1, :]
                else:
                    act.wait_ge(act_done, UN * m + k + 1)
                    bank = psum[:, HID0 + (k if kind == OLD else k - (UN - KC)) % 2, :]
                if k >= 2:
                    act.wait_ge(out_unit_done, (UN - 1) * m + k - 1)
                elif k == 1:
                    wait(act, out_done, G * m)
                else:
                    wait(act, out_unit_done, (UN - 1) * m)
                act.activation(hid_hi[:, k % 2], bank, ACT.Copy).then_inc(hid_hi_done, 1)

            def bias_rows_high(q):
                act.wait_ge(brow_loaded, 32 * (q + 1))
                act.activation(brow_hi[:], brow_raw[:], ACT.Copy).then_inc(brow_hi_done, 1)

            def y_normalise(m, js):
                for j in js:
                    act.wait_ge(y_scaled, G * m + j + 1)
                    bank = psum[:, OUT0 + j, :]
                    act.activation(bank, bank, ACT.Identity, bias=y_sc[:, 1, j:j + 1],
                                   scale=y_sc[:, 0, j:j + 1]).then_inc(y_normed, 1)

            act.wait_ge(consts_loaded, 16 * 8)
            act.activation(bsel[:], bsel_raw[:], ACT.Copy).then_inc(bsel_done, 1)
            xt_high(0, range(G))
            bias_rows_high(0)
            pieces_high(0, 0, 0, 0, -1)

            def step(m, q, hf, par):
                if not first(m):
                    y_normalise(m - 1, (0,))
                for k in range(UN):
                    activate(m, q, k)
                    hidden_high(m, k)
                    if k == 0 and not first(m):
                        y_normalise(m - 1, (1, 2, 3))
                    pieces_high(m, q, hf, par, k)
                    if k == 4 and hf == 1 and not is_last(m):
                        bias_rows_high(q + 1)
                if not is_last(m):
                    xt_high(m + 1, range(G))

            steps(act, step)
            y_normalise(2 * NQ - 1, range(G))

        @block.vector
        def _(dve):
            def x_statistics(m, q, hf):
                dve.wait_ge(x1_loaded[hf], 16 * (q + 1))
                wait(dve, x_stats, G * m)
                wait(dve, xn_done, G * m)
                for j in range(G):
                    dve.bn_stats(x_bn[:, j], x1[:, hf, j]).then_inc(x_bn_done, 1)
                for j in range(G):
                    dve.wait_ge(x_bn_done, G * m + j + 1)
                    after_wait(dve)
                    dve.bn_aggr(x_mv[:, j], x_bn[:, j]).then_inc(x_stats, 1)

            def xt_low(m, js):
                for j in js:
                    dve.wait_ge(xt_hi_done, G * m + j + 1)
                    at = slice(j * P, (j + 1) * P)
                    dve.tensor_tensor(xt_lo[:, :, at], psum[:, j % 2, :].rearrange("p (c q) -> p c q", c=KC),
                                      xt_hi[:, :, at].bitcast(F32), ALU.subtract).then_inc(xt_lo_done, 1)

            def pieces_low(m, q, hf, par, k):
                for n, (w_hi, w_lo, scale) in pieces_after(m, q, hf, par, k):
                    slot = n % RING if isinstance(n, int) else (k - 5) % RING
                    dve.wait_ge(piece_hi_done, n + 1)
                    dve.scalar_tensor_tensor(w_lo, stage[:, slot], scale, w_hi.bitcast(F32), ALU.mult,
                                             ALU.subtract).then_inc(piece_lo_done, 1)

            def product(m, k):
                if kinds[k] != SHARED:
                    return
                bank = psum[:, HID0 + 1, :]
                dve.wait_ge(hid_mm_done, HM * m + starts[k] + 2)
                dve.wait_ge(act_done, UN * m + k + 1)
                dve.scalar_tensor_tensor(bank, bank, b_s3[:, k - KC:k - KC + 1], gate[:], ALU.add,
                                         ALU.mult).then_inc(prod_done, 1)

            def hidden_low(m, k):
                kind = kinds[k]
                bank = psum[:, HID0 + (1 if kind == SHARED else (k if kind == OLD else k - (UN - KC)) % 2), :]
                dve.wait_ge(hid_hi_done, UN * m + k + 1)
                dve.tensor_tensor(hid_lo[:, k % 2], bank, hid_hi[:, k % 2].bitcast(F32),
                                  ALU.subtract).then_inc(hid_lo_done, 1)

            def bias_rows(q):
                dve.wait_ge(brow_hi_done, q + 1)
                if not (isinstance(q, int) and q == 0):
                    dve.wait_ge(out_unit_done, 2 * (UN - 1) * q - (UN - 1) + 1)
                dve.scalar_tensor_tensor(brow[:], brow_hi[:].bitcast(F32), low_rows[:, 0:1], brow_raw[:],
                                         ALU.mult, ALU.add).then_inc(brow_done, 1)

            def y_stat(m, j):
                bank = psum[:, OUT0 + j, :]
                dve.wait_ge(out_done, G * m + j + 1)
                dve.bn_stats(y_bn[:, j], bank).then_inc(y_bn_done, 1)
                dve.wait_ge(y_bn_done, G * m + j + 1)
                after_wait(dve)
                dve.bn_aggr(y_mv[:, j], y_bn[:, j]).then_inc(y_stats, 1)

            def y_add(m, hf, j):
                dve.wait_ge(y_normed, G * m + j + 1)
                dve.tensor_tensor(x1[:, hf, j], psum[:, OUT0 + j, :], x1[:, hf, j], ALU.add).then_inc(x2_ready, 1)

            dve.wait_ge(consts_loaded, 16 * 8)
            x_statistics(0, 0, 0)
            xt_low(0, range(G))
            bias_rows(0)
            pieces_low(0, 0, 0, 0, -1)

            def step(m, q, hf, par):
                prev = 1 - hf
                if not first(m):
                    for j in range(G):
                        y_stat(m - 1, j)
                    y_add(m - 1, prev, 0)
                for k in range(UN):
                    product(m, k)
                    hidden_low(m, k)
                    if k == 0 and not first(m):
                        for j in range(1, G):
                            y_add(m - 1, prev, j)
                    pieces_low(m, q, hf, par, k)
                    if k == 4 and hf == 1 and not is_last(m):
                        bias_rows(q + 1)
                    if k == 10 and not is_last(m):
                        x_statistics(m + 1, q if hf == 0 else q + 1, 1 - hf)
                if not is_last(m):
                    xt_low(m + 1, range(G))

            steps(dve, step)
            for j in range(G):
                y_stat(2 * NQ - 1, j)
            for j in range(G):
                y_add(2 * NQ - 1, 1, j)



def lay_out(inputs):
    import numpy as np

    def rows(w):
        return np.ascontiguousarray(w.reshape(-1, P, w.shape[-1]).transpose(1, 0, 2))

    def cols(v):
        return np.ascontiguousarray(v.reshape(-1, P).T)

    a = {k.removeprefix("L0_"): np.asarray(v) for k, v in inputs.items()}
    gate_b = np.concatenate([a["attn_b_gx"].reshape(HC, 64), a["attn_b_ga"].reshape(HC, 64)], axis=1).T
    return {
        "x": np.ascontiguousarray(a["attn_x"].reshape(N, D)),
        "w_in": rows(a["attn_w_in"]),
        "b_in": cols(a["attn_b_in"]),
        "w_gate": np.ascontiguousarray(np.concatenate([a["attn_w_gx"], a["attn_w_ga"]], axis=2).transpose(1, 0, 2)),
        "b_gate": np.ascontiguousarray(gate_b),
        "a_real": cols(a["attn_a_real_param"]),
        "a_imag": cols(a["attn_a_imag_param"]),
        "w_out": rows(a["attn_w_out"]),
        "b_out": np.ascontiguousarray(np.stack([a["attn_b_out"]] * 2)),
        "low_row": np.array([[0.0], [-1.0]], np.float32),
        "ident": np.eye(P, dtype=np.float32),
        "sw1": a["ffn_sw1"], "sw3": a["ffn_sw3"], "sw2": a["ffn_sw2"], "w1": a["ffn_w1"], "w2": a["ffn_w2"],
        "b_s1": cols(a["ffn_sb1"]),
        "b_s3": cols(a["ffn_sb3"]),
        "b_s2": np.ascontiguousarray(a["ffn_sb2"].reshape(1, D)),
        "b_r1": cols(np.concatenate([a["ffn_b1"][-j % NE] for j in range(NE + 1)])),
        "b_r2": np.ascontiguousarray(np.stack([a["ffn_b2"][-j % NE] for j in range(NE + 1)])),
        "bsel": np.repeat(np.array([[1.0], [0.5], [0.5]] * 2, np.float32), P, axis=1),
        "low_rows": np.repeat(np.array([[0.0], [-1.0]], np.float32), 3, axis=0),
    }


def sandwich(nc, d):
    d["x1"] = nc.dram_tensor("x1_rows", (N, D), F32).ap()
    phase_a(nc, d)
    phase_b(nc, d)


def kernel(**inputs):
    import concourse.bacc as bacc
    from concourse.bass_utils import run_bass_kernel_spmd

    nc = bacc.Bacc("TRN2", target_bir_lowering=False, num_devices=1, dynamic_dma_scratch_size=1024)
    arrays = {f"in_{k}": v for k, v in lay_out(inputs).items()}
    d = {k[3:]: nc.dram_tensor(k, v.shape, F32, kind="ExternalInput").ap() for k, v in arrays.items()}
    d["out"] = nc.dram_tensor("out_rows", (N, D), F32, kind="ExternalOutput").ap()
    sandwich(nc, d)
    r = run_bass_kernel_spmd(nc, [arrays], core_ids=[0])
    return r.results[0]["out_rows"].reshape(B, S, D)
```

```python
from contextlib import ExitStack
import math

import concourse.bass as bass
from concourse import mybir

F32 = mybir.dt.float32
F32R = mybir.dt.float32r
ALU = mybir.AluOpType
ACT = mybir.ActivationFunctionType

P = 128
B, S, D = 4, 2048, 512
N = B * S
DH = 1024
KC = D // P
HC = DH // P
T = 512
G = T // P
NT = N // T
TPB = S // T
NE = 8
EPS = 1e-5
MAGIC = 1.5 * 2 ** 23
TWO_PI = 2 * math.pi
LOG_A_SCALE = -8.0
TWO_PI_SAFE = 6.283185
HS = 1024
HR = 512
RING = 4


def wait(eng, sem, n):
    if isinstance(n, int) and n <= 0:
        return
    eng.wait_ge(sem, n)


def after_wait(eng):
    eng.nop(nofuse=True)


class Shared:

    def __init__(self, nc, ctx):
        def sb(name, shape, dt=F32):
            return ctx.enter_context(nc.sbuf_tensor(name, shape, dt))

        def sem(name):
            return ctx.enter_context(nc.semaphore(name))

        self.rows = sb("rows", [P, 2, G, D])
        self.xn = sb("xn", [P, G, D])
        self.xt_hi = sb("xt_hi", [P, KC, T], F32R)
        self.xt_lo = sb("xt_lo", [P, KC, T], F32R)
        self.w_hi = sb("w_hi", [P, KC, DH], F32R)
        self.w_lo = sb("w_lo", [P, KC, DH], F32R)
        self.stage = sb("stage", [P, RING, D])
        self.ident = sb("ident", [P, P])
        self.neg_half = sb("neg_half", [P, G])
        self.x_bn = sb("x_bn", [P, G, 6])
        self.x_mv = sb("x_mv", [P, G, 2])
        self.x_sc = sb("x_sc", [P, 2, G])
        self.y_bn = sb("y_bn", [P, G, 6])
        self.y_mv = sb("y_mv", [P, G, 2])
        self.y_sc = sb("y_sc", [P, 2, G])
        self.psum = ctx.enter_context(nc.psum_tensor("psum", [P, 8, 512], F32))
        self.bsel_raw = sb("bsel_raw", [6, P])
        self.low_rows = sb("low_rows", [6, 1])
        self.b_s1, self.b_s3 = sb("b_s1", [P, HS // P]), sb("b_s3", [P, HS // P])
        self.b_r1 = sb("b_r1", [P, (NE + 1) * KC])
        self.x1_stored = sem("x1_stored")
        self.y_stats = sem("y_stats")
        self.y_small = sem("y_small")
        self.y_scaled = sem("y_scaled")
        self.y_normed = sem("y_normed")
        self.x1_ready = sem("x1_ready")
        self.last_out_banks = (0, 1, 6, 7)
        self.x1_loaded = [sem(f"f_x1_loaded{k}") for k in range(2)]
        self.piece_loaded = [sem(f"f_piece_loaded{k}") for k in range(RING)]
        self.piece_hi_done = sem("f_piece_hi_done")
        self.piece_lo_done = sem("f_piece_lo_done")
        self.x_bn_done = sem("f_x_bn_done")
        self.x_stats = sem("f_x_stats")
        self.x_small = sem("f_x_small")
        self.xn_done = sem("f_xn_done")
        self.transposed = sem("f_transposed")
        self.xt_hi_done = sem("f_xt_hi_done")
        self.xt_lo_done = sem("f_xt_lo_done")
        self.consts_loaded = sem("f_consts_loaded")
        self.brow_loaded = sem("f_brow_loaded")


def ffn_w1(shared):
    return [w[:].rearrange("p k n -> p (k n)").rearrange("p (s k n) -> p s k n", s=2, k=KC)
            for w in (shared.w_hi, shared.w_lo)]


def ffn_bias_rows(shared):
    return shared.xn[0:6, 3]


def ffn_rows(tensor, q, hf):
    rows = tensor.rearrange("(g p r) d -> r p g d", p=P, r=NE)
    at = slice(hf * G, (hf + 1) * G)
    if isinstance(q, int):
        return rows[5 * q % NE, :, at]
    return rows[bass.ds(5 * q % NE, 1), :, at].rearrange("o p g d -> p (o g) d")


def phase_a(nc, d, shared, NT=NT):
    with ExitStack() as ctx:
        def sb(name, shape, dt=F32):
            return ctx.enter_context(nc.sbuf_tensor(name, shape, dt))

        def sem(name):
            return ctx.enter_context(nc.semaphore(name))

        win_hi, win_lo = shared.w_hi, shared.w_lo
        wgate = sb("wgate", [P, HC, P])
        wout = sb("wout", [P, HC, D])
        x_in = shared.rows[:, 0]
        x_res = shared.rows[:, 1]
        xn, xt_hi, xt_lo = shared.xn, shared.xt_hi, shared.xt_lo
        xh = sb("xh", [P, 2, KC, T])
        tanh_x = sb("tanh_x", [P, KC, T])
        tanh_a = sb("tanh_a", [P, KC, T])
        mag = sb("mag", [P, KC, T])
        gain = sb("gain", [P, KC, T])
        turns = sb("turns", [P, KC, T])
        frac = sb("frac", [P, KC, T])
        sin = sb("sin", [P, KC, T])
        cos = sb("cos", [P, KC, T])
        h = sb("h", [P, 2, KC, T])
        cross = sb("cross", [P, 2, KC, T])
        ones = sb("ones", [P, T])
        ident = shared.ident
        bout_raw = sb("bout_raw", [2, D])
        bout_hi = sb("bout_hi", [2, D], F32R)
        bout = sb("bout", [2, D], F32R)
        low_row = sb("low_row", [2, 1])
        ones_row = sb("ones_row", [2, P], F32R)
        b_in = sb("b_in", [P, HC])
        b_gate = sb("b_gate", [P, HC])
        a_real = sb("a_real", [P, KC])
        a_imag = sb("a_imag", [P, KC])
        half_turn = sb("half_turn", [P, KC])
        sp = sb("sp", [P, 6, KC])
        mag_k = sb("mag_k", [P, KC])
        mag2_k = sb("mag2_k", [P, KC])
        halfpi = sb("halfpi", [P, 1])
        keep = sb("keep", [P, NT + 1])
        carry = sb("carry", [P, 2, KC])
        neg_half, x_bn, x_mv, x_sc = shared.neg_half, shared.x_bn, shared.x_mv, shared.x_sc
        y_bn, y_mv, y_sc = shared.y_bn, shared.y_mv, shared.y_sc
        psum = shared.psum
        OUT0 = 4

        consts_loaded = sem("consts_loaded")
        win_loaded = sem("win_loaded")
        wout_loaded = sem("wout_loaded")
        win_hi_done = sem("win_hi_done")
        win_lo_done = sem("win_lo_done")
        pool_consts = sem("pool_consts")
        dve_consts = sem("dve_consts")
        dve_small = sem("dve_small")
        act_small = sem("act_small")
        xin_loaded = sem("xin_loaded")
        xres_loaded = sem("xres_loaded")
        x1_stored = shared.x1_stored
        x_stats = sem("x_stats")
        x_bn_done = sem("x_bn_done")
        xn_done = sem("xn_done")
        x_small = sem("x_small")
        y_small = shared.y_small
        transposed = sem("transposed")
        xt_hi_done = sem("xt_hi_done")
        xt_lo_done = sem("xt_lo_done")
        win_done = sem("win_done")
        xh_done = sem("xh_done")
        gate_mm_done = sem("gate_mm_done")
        tanh_done = sem("tanh_done")
        inc_done = sem("inc_done")
        turns_done = sem("turns_done")
        round_done = sem("round_done")
        frac_done = sem("frac_done")
        mag_done = sem("mag_done")
        mag2_done = sem("mag2_done")
        z_done = sem("z_done")
        norm_done = sem("norm_done")
        gain_done = sem("gain_done")
        sin_done = sem("sin_done")
        abs_done = sem("abs_done")
        cos_done = sem("cos_done")
        gsin_done = sem("gsin_done")
        gcos_done = sem("gcos_done")
        cross_done = sem("cross_done")
        cross_pool_done = sem("cross_pool_done")
        fwd_mul_done = sem("fwd_mul_done")
        back_cross_done = sem("back_cross_done")
        back_pool_done = sem("back_pool_done")
        fwd_done = sem("fwd_done")
        scan_done = sem("scan_done")
        back_mul_done = sem("back_mul_done")
        h_done = sem("h_done")
        carry_done = sem("carry_done")
        out_done = sem("out_done")
        y_bn_done = sem("y_bn_done")
        y_stats = shared.y_stats
        y_scaled = shared.y_scaled
        y_normed = shared.y_normed
        x1_ready = shared.x1_ready

        x_rows = d["x"].rearrange("(t g p) d -> t p g d", g=G, p=P)
        x1_rows = d["x1"].rearrange("(t g p) d -> t p g d", g=G, p=P)
        LAST = NT - 1
        POOL_CHUNKS, DVE_CHUNKS = (0,), (1, 2, 3)
        SERVED = DVE_CHUNKS + POOL_CHUNKS
        ORDER = (1, 5, 2, 6, 3, 7, 0, 4)
        PROJECT, GATES = range(2)
        LEAD = 4
        RINGED = [(PROJECT, n) for n in ORDER[:LEAD]]
        for k in range(HC - LEAD):
            RINGED += [(GATES, ORDER[k]), (PROJECT, ORDER[k + LEAD])]
        RINGED += [(GATES, n) for n in ORDER[HC - LEAD:]]

        def tile_of(rows, t):
            if isinstance(t, int):
                return rows[t]
            return rows[bass.ds(t, 1)].rearrange("o p g d -> p (o g) d")

        def steps(eng, step):
            step(0)
            with eng.Fori(0, (NT - 2) // 2) as i:
                for u in range(2):
                    step(2 * i + (1 + u))
            step(LAST)

        def out_bank(t, j):
            return psum[:, shared.last_out_banks[j] if last(t) else OUT0 + j, :]

        FFN_BANKS = (2, 3, 4, 5)

        def first(t):
            return isinstance(t, int) and t == 0

        def last(t):
            return isinstance(t, int) and t == LAST

        block = ctx.enter_context(nc.Block())

        @block.sync
        def _(sp_):
            sp_.dma_start(x_in, tile_of(x_rows, 0)).then_inc(xin_loaded, 16)
            sp_.dma_start(h[:].rearrange("p a c t -> p (a c t)"),
                          d["w_in"].rearrange("p k n -> p (k n)")).then_inc(win_loaded, 16)
            for dst, src in ((b_in, "b_in"), (b_gate, "b_gate"), (a_real, "a_real"), (a_imag, "a_imag"),
                             (ident, "ident"), (bout_raw, "b_out"), (low_row, "low_row")):
                sp_.dma_start(dst[:], d[src]).then_inc(consts_loaded, 16)
            sp_.dma_start(wgate[:], d["w_gate"]).then_inc(consts_loaded, 16)
            sp_.dma_start(wout[:], d["w_out"]).then_inc(wout_loaded, 16)
            sp_.dma_start(x_res, tile_of(x_rows, 0)).then_inc(xres_loaded, 16)
            sp_.wait_ge(xn_done, G)
            sp_.dma_start(x_in, tile_of(x_rows, 1)).then_inc(xin_loaded, 16)

            def step(t):
                if not first(t):
                    sp_.wait_ge(x1_ready, G * t)
                    after_wait(sp_)
                    sp_.dma_start(tile_of(x1_rows, t - 1), x_res).then_inc(x1_stored, 16)
                    sp_.wait_ge(x1_stored, 16 * t)
                    after_wait(sp_)
                    sp_.dma_start(x_res, tile_of(x_rows, t)).then_inc(xres_loaded, 16)

            def step_in(t):
                sp_.wait_ge(xn_done, G * (t + 2))
                after_wait(sp_)
                sp_.dma_start(x_in, tile_of(x_rows, t + 2)).then_inc(xin_loaded, 16)

            step_in(0)
            with sp_.Fori(0, (NT - 2) // 2 - 1) as i:
                for u in range(2):
                    step_in(2 * i + (1 + u))
                    step(2 * i + (1 + u))
            step_in(NT - 3)
            step(NT - 3)
            step(NT - 2)
            sp_.wait_ge(xn_done, G * NT)
            sp_.wait_ge(x1_stored, 16 * (NT // 2))
            sp_.dma_start(x_in, ffn_rows(d["x1"], 0, 0)).then_inc(shared.x1_loaded[0], 16)
            for k in range(KC):
                sp_.dma_start(shared.stage[:, k], d["w1"].rearrange("e (k p) n -> e k p n", p=P)[0, k]).then_inc(
                    shared.piece_loaded[k], 16)
            for dst, src in ((shared.bsel_raw, "bsel"), (shared.low_rows, "low_rows"), (shared.b_s1, "b_s1"),
                             (shared.b_s3, "b_s3"), (shared.b_r1, "b_r1")):
                sp_.dma_start(dst[:], d[src]).then_inc(shared.consts_loaded, 16)
            step(LAST)
            sp_.wait_ge(shared.transposed, G)
            brow_raw = ffn_bias_rows(shared)
            for at in (0, 3):
                sp_.dma_start(brow_raw[at:at + 1, :], d["b_s2"]).then_inc(shared.consts_loaded, 16)
                sp_.dma_start(brow_raw[at + 1:at + 3, :], d["b_r2"][0:2]).then_inc(shared.brow_loaded, 16)
            for k in range(KC):
                sp_.wait_ge(shared.piece_lo_done, k + 1)
                sp_.dma_start(shared.stage[:, k], d["w2"].rearrange("e (k p) n -> e k p n", p=P)[0, k]).then_inc(
                    shared.piece_loaded[k], 16)

        @block.gpsimd
        def _(pool):
            pool.memset(neg_half[:], -0.5).then_inc(pool_consts, 1)
            pool.wait_ge(pool_consts, 1)

            def scales(mv, sc, small, n, done):
                after_wait(pool)
                pool.tensor_scalar(sc[:, 0], mv[:, :, 1], EPS, 1.0, ALU.add, ALU.mult).then_inc(small, 1)
                pool.tensor_scalar(sc[:, 1], mv[:, :, 0], -1.0, 0.0, ALU.mult, ALU.add).then_inc(small, 1)
                pool.wait_ge(small, n + 2)
                w = sc.shape[-1]
                pool.tensor_tensor(sc[:, 0], sc[:, 0], neg_half[:, 0:w], ALU.pow).then_inc(small, 1)
                pool.wait_ge(small, n + 3)
                pool.tensor_tensor(sc[:, 1], sc[:, 1], sc[:, 0], ALU.mult).then_inc(done, 1)

            def scale_x(t):
                pool.wait_ge(x_stats, G * (t + 1))
                wait(pool, xn_done, G * t)
                scales(x_mv[:], x_sc[:], x_small, 4 * t, x_small)

            def scale_y(t):
                pool.wait_ge(y_stats, G * (t + 1))
                wait(pool, y_normed, G * t)
                scales(y_mv[:], y_sc[:], y_small, 3 * t, y_scaled)

            def both(plane, c):
                return plane[:, c:c + 1, :].to_broadcast([P, 2, T])

            def cross_products(t):
                for c in POOL_CHUNKS:
                    pool.wait_ge(gsin_done, KC * t + c + 1)
                    wait(pool, h_done, 2 * KC * t)
                    pool.tensor_tensor(cross[:, :, c], xh[:, :, c], both(turns, c), ALU.mult).then_inc(
                        cross_pool_done, 1)

            def back_cross_products(t):
                for c in POOL_CHUNKS:
                    pool.wait_ge(scan_done, 2 * (KC * t + c + 1))
                    pool.tensor_tensor(cross[:, :, c], h[:, :, c], both(sin, c), ALU.mult).then_inc(
                        back_pool_done, 1)

            scale_x(0)
            scale_x(1)

            def step(t):
                cross_products(t)
                if last(t):
                    back_cross_products(t)
                if not first(t):
                    scale_y(t - 1)
                if not (isinstance(t, int) and t >= NT - 2):
                    scale_x(t + 2)
                if not last(t):
                    back_cross_products(t)

            step(0)
            with pool.Fori(0, (NT - 2) // 2 - 1) as i:
                for u in range(2):
                    step(2 * i + (1 + u))
            step(NT - 3)
            step(NT - 2)
            step(LAST)
            pool.wait_ge(shared.x_stats, G)
            pool.wait_ge(xn_done, G * NT)
            scales(x_mv[:], x_sc[:], shared.x_small, 0, shared.x_small)
            pool.wait_ge(shared.x_small, 4)
            pool.wait_ge(transposed, G * NT)
            for j in range(G):
                pool.tensor_scalar(xn[:, j], x_in[:, j], x_sc[:, 0, j:j + 1], x_sc[:, 1, j:j + 1],
                                   ALU.mult, ALU.add).then_inc(shared.xn_done, 1)

        @block.tensor
        def _(pe):
            def transposes(t, js):
                for j in js:
                    pe.wait_ge(xn_done, G * t + j + 1)
                    evacuated(t - 1, len(RINGED) - 4 + j)
                    for c in range(KC):
                        mm = pe.transpose(psum[:, j, c * P:(c + 1) * P], xn[:, j, c * P:(c + 1) * P], ident[:])
                    mm.then_inc(transposed, 1)

            def evacuated(t, r):
                kind, n = RINGED[r]
                if kind == PROJECT:
                    wait(pe, xh_done, HC * t + (ORDER.index(n) + 1) if not before_first(t) else 0)
                else:
                    wait(pe, tanh_done, 2 * (HC * t + (ORDER.index(n) + 1)) if not before_first(t) else 0)

            def before_first(t):
                return isinstance(t, int) and t < 0

            def project_and_gates(t):
                for r, (kind, n) in enumerate(RINGED):
                    bank = psum[:, r % 4, :]
                    if r < 4:
                        if r == 0:
                            pe.wait_ge(xt_lo_done, G * (t + 1))
                    else:
                        evacuated(t, r - 4)
                    if kind == PROJECT:
                        for kc in range(KC):
                            w_hi = win_hi[:, kc, n * P:(n + 1) * P]
                            w_lo = win_lo[:, kc, n * P:(n + 1) * P]
                            pe.matmul(bank, w_hi, xt_hi[:, kc], start=(kc == 0), stop=False)
                            pe.matmul(bank, w_hi, xt_lo[:, kc], start=False, stop=False)
                            mm = pe.matmul(bank, w_lo, xt_hi[:, kc], start=False, stop=(kc == KC - 1))
                        mm.then_inc(win_done, 1)
                    else:
                        pe.wait_ge(xh_done, HC * t + (ORDER.index(n) + 1))
                        pe.matmul(bank, wgate[:, n], xh[:, n // KC, n % KC],
                                  start=True, stop=True).then_inc(gate_mm_done, 1)

            def out_project(t, js=range(G)):
                for j in js:
                    if j == 0:
                        pe.wait_ge(h_done, 2 * KC * (t + 1))
                    bank = out_bank(t, j)
                    pe.matmul(bank, ones_row[:], bout[:], start=True, stop=False)
                    for k in range(HC):
                        mm = pe.matmul(bank, h[:, k // KC, k % KC, j * P:(j + 1) * P], wout[:, k],
                                       start=False, stop=(k == HC - 1))
                    mm.then_inc(out_done, 1)

            pe.wait_ge(consts_loaded, 16 * 8)
            transposes(0, range(G))
            pe.wait_ge(win_hi_done, KC)
            pe.wait_ge(win_lo_done, KC)
            project_and_gates(0)

            def step(t):
                if not last(t):
                    transposes(t + 1, (0, 1, 2))
                if not first(t):
                    out_project(t - 1, (0,))
                if not last(t):
                    transposes(t + 1, (3,))
                if not first(t):
                    out_project(t - 1, (1, 2, 3))
                if not last(t):
                    project_and_gates(t + 1)
                if first(t):
                    pe.wait_ge(wout_loaded, 16)
                    pe.wait_ge(dve_consts, 4)

            steps(pe, step)
            pe.wait_ge(tanh_done, 2 * HC * NT)
            out_project(LAST, (0, 1))
            pe.wait_ge(x1_ready, G * LAST)
            for j in range(G):
                pe.wait_ge(shared.xn_done, j + 1)
                for c in range(KC):
                    mm = pe.transpose(psum[:, FFN_BANKS[j], c * P:(c + 1) * P], xn[:, j, c * P:(c + 1) * P],
                                      ident[:])
                mm.then_inc(shared.transposed, 1)
            out_project(LAST, (2, 3))

        @block.scalar
        def _(act):
            def normalise(t):
                for j in range(G):
                    act.wait_ge(x_small, 4 * t + 4)
                    wait(act, transposed, G * t)
                    act.activation(xn[:, j], x_in[:, j], ACT.Identity, bias=x_sc[:, 1, j:j + 1],
                                   scale=x_sc[:, 0, j:j + 1]).then_inc(xn_done, 1)

            normalise(0)
            act.wait_ge(win_loaded, 16)
            hw = h[:].rearrange("p a c t -> p (a c t)").rearrange("p (k n) -> p k n", k=KC)
            for kc in range(KC):
                act.activation(win_hi[:, kc], hw[:, kc], ACT.Copy).then_inc(win_hi_done, 1)
            act.wait_ge(consts_loaded, 16 * 8)
            act.activation(sp[:, 0], a_real[:], ACT.Abs).then_inc(act_small, 1)
            act.activation(bout_hi[:], bout_raw[:], ACT.Copy).then_inc(act_small, 1)
            act.wait_ge(act_small, 2)
            act.activation(sp[:, 1], sp[:, 0], ACT.Exp, scale=-1.0).then_inc(act_small, 1)

            def xt_high(t, js):
                for j in js:
                    act.wait_ge(transposed, G * t + j + 1)
                    if j == 0:
                        wait(act, win_done, HC * t)
                    act.activation(xt_hi[:, :, j * P:(j + 1) * P],
                                   psum[:, j, :].rearrange("p (c q) -> p c q", c=KC),
                                   ACT.Copy).then_inc(xt_hi_done, 1)

            def evacuate(t, part):
                for r, (kind, n) in list(enumerate(RINGED))[part]:
                    bank = psum[:, r % 4, :]
                    k = ORDER.index(n)
                    if kind == PROJECT:
                        act.wait_ge(win_done, HC * t + k + 1)
                        wait(act, fwd_done, 2 * (KC * (t - 1) + SERVED.index(n % KC) + 1))
                        act.activation(xh[:, n // KC, n % KC], bank, ACT.Identity,
                                       bias=b_in[:, n:n + 1]).then_inc(xh_done, 1)
                        continue
                    act.wait_ge(gate_mm_done, HC * t + k + 1)
                    if k == 0:
                        wait(act, gain_done, KC * t)
                        wait(act, mag_done, KC * t)
                        wait(act, inc_done, KC * t)
                    to = slice(64 * (n % 2), 64 * (n % 2) + 64)
                    act.activation(tanh_x[to, n // 2], bank[0:64], ACT.Tanh,
                                   bias=b_gate[0:64, n:n + 1], scale=0.5).then_inc(tanh_done, 1)
                    act.activation(tanh_a[to, n // 2], bank[64:128], ACT.Tanh,
                                   bias=b_gate[64:128, n:n + 1], scale=0.5).then_inc(tanh_done, 1)

            def exps(t):
                act.wait_ge(tanh_done, 2 * HC * (t + 1))
                for c in range(KC):
                    wait(act, fwd_mul_done, KC * t)
                    act.activation(turns[:, c], tanh_a[:, c], ACT.Identity, bias=half_turn[:, c:c + 1],
                                   scale=half_turn[:, c:c + 1]).then_inc(inc_done, 1)
                for c in range(KC):
                    wait(act, gcos_done, KC * t)
                    act.activation(gain[:, c], tanh_a[:, c], ACT.Exp, bias=mag2_k[:, c:c + 1],
                                   scale=mag2_k[:, c:c + 1]).then_inc(mag2_done, 1)

            def mags(t):
                for c in range(KC):
                    wait(act, scan_done, 2 * (KC * (t - 1) + c + 1))
                    act.activation(mag[:, c], tanh_a[:, c], ACT.Exp, bias=mag_k[:, c:c + 1],
                                   scale=mag_k[:, c:c + 1]).then_inc(mag_done, 1)

            def norm_roots(t):
                for c in range(KC):
                    act.wait_ge(z_done, KC * t + c + 1)
                    act.activation(gain[:, c], gain[:, c], ACT.Sqrt, scale=-0.25).then_inc(norm_done, 1)

            def sines(t):
                for c in range(KC):
                    act.wait_ge(frac_done, KC * t + c + 1)
                    wait(act, back_mul_done, KC * t)
                    act.activation(sin[:, c], frac[:, c], ACT.Sin, scale=-TWO_PI_SAFE).then_inc(sin_done, 1)
                for c in range(KC):
                    act.activation(cos[:, c], frac[:, c], ACT.Abs).then_inc(abs_done, 1)
                for c in range(KC):
                    act.wait_ge(abs_done, KC * t + c + 1)
                    act.activation(cos[:, c], cos[:, c], ACT.Sin, bias=halfpi[:, 0:1],
                                   scale=-TWO_PI_SAFE).then_inc(cos_done, 1)

            def y_normalise(t):
                for j in range(G):
                    act.wait_ge(y_scaled, t + 1)
                    act.activation(psum[:, OUT0 + j, :], psum[:, OUT0 + j, :], ACT.Identity,
                                   bias=y_sc[:, 1, j:j + 1], scale=y_sc[:, 0, j:j + 1]).then_inc(y_normed, 1)

            xt_high(0, range(G))
            normalise(1)
            act.wait_ge(dve_consts, 4)
            evacuate(0, slice(None))

            def step(t):
                if not last(t):
                    xt_high(t + 1, (0, 1, 2))
                exps(t)
                if not last(t):
                    xt_high(t + 1, (3,))
                norm_roots(t)
                sines(t)
                mags(t)
                if not last(t):
                    evacuate(t + 1, slice(0, 1))
                if not first(t):
                    y_normalise(t - 1)
                if not last(t):
                    evacuate(t + 1, slice(1, 6))
                if not (isinstance(t, int) and t >= NT - 2):
                    normalise(t + 2)
                if not last(t):
                    evacuate(t + 1, slice(6, None))

            step(0)
            with act.Fori(0, (NT - 2) // 2 - 1) as i:
                for u in range(2):
                    step(2 * i + (1 + u))
            step(NT - 3)
            step(NT - 2)
            step(LAST)
            act.wait_ge(win_done, HC * NT)
            act.wait_ge(win_lo_done, KC)
            w1_hi, _ = ffn_w1(shared)
            for k in range(KC):
                act.wait_ge(shared.piece_loaded[k], 16)
                act.activation(w1_hi[:, 0, k], shared.stage[:, k], ACT.Copy).then_inc(shared.piece_hi_done, 1)
            act.wait_ge(xt_lo_done, G * NT)
            for j in range(G):
                act.wait_ge(shared.transposed, j + 1)
                act.activation(xt_hi[:, :, j * P:(j + 1) * P],
                               psum[:, FFN_BANKS[j], :].rearrange("p (c q) -> p c q", c=KC),
                               ACT.Copy).then_inc(shared.xt_hi_done, 1)

        @block.vector
        def _(dve):
            def x_statistics(t):
                dve.wait_ge(xin_loaded, 16 * (t + 1))
                wait(dve, x_stats, G * t)
                wait(dve, xn_done, G * t)
                for j in range(G):
                    dve.bn_stats(x_bn[:, j], x_in[:, j]).then_inc(x_bn_done, 1)
                for j in range(G):
                    dve.wait_ge(x_bn_done, G * t + j + 1)
                    after_wait(dve)
                    dve.bn_aggr(x_mv[:, j], x_bn[:, j]).then_inc(x_stats, 1)

            def xt_low(t, js):
                for j in js:
                    dve.wait_ge(xt_hi_done, G * t + j + 1)
                    at = slice(j * P, (j + 1) * P)
                    dve.tensor_tensor(xt_lo[:, :, at], psum[:, j, :].rearrange("p (c q) -> p c q", c=KC),
                                      xt_hi[:, :, at].bitcast(F32), ALU.subtract).then_inc(xt_lo_done, 1)

            dve.memset(ones[:], 1.0).then_inc(dve_consts, 1)
            dve.memset(halfpi[:], math.pi / 2).then_inc(dve_consts, 1)
            dve.memset(carry[:], 0.0).then_inc(carry_done, 1)
            dve.memset(keep[:], 1.0).then_inc(dve_small, 1)
            dve.wait_ge(dve_small, 1)
            dve.memset(keep[:, 0:NT + 1:TPB], 0.0).then_inc(dve_small, 1)
            x_statistics(0)
            dve.wait_ge(dve_consts, 1)
            dve.tensor_copy(ones_row[:], ones[0:2, 0:P]).then_inc(dve_consts, 1)
            hw = h[:].rearrange("p a c t -> p (a c t)").rearrange("p (k n) -> p k n", k=KC)
            for kc in range(KC):
                dve.wait_ge(win_hi_done, kc + 1)
                dve.tensor_tensor(win_lo[:, kc], hw[:, kc], win_hi[:, kc].bitcast(F32),
                                  ALU.subtract).then_inc(win_lo_done, 1)
            xt_low(0, range(G))
            small = [2]

            def link(ins):
                small[0] += 1
                ins.then_inc(dve_small, 1)
                dve.wait_ge(dve_small, small[0])

            dve.wait_ge(act_small, 3)
            link(dve.scalar_tensor_tensor(bout[:], bout_hi[:].bitcast(F32), low_row[:, 0:1], bout_raw[:],
                                          ALU.mult, ALU.add))
            link(dve.tensor_scalar(b_gate[:], b_gate[:], 0.5, None, ALU.mult))
            link(dve.tensor_scalar(half_turn[:], a_imag[:], 1 / (4 * math.pi), None, ALU.mult))
            link(dve.tensor_scalar(sp[:, 2], sp[:, 1], 2.0, None, ALU.add))
            link(dve.reciprocal(sp[:, 3], sp[:, 2]))
            link(dve.tensor_tensor(sp[:, 3], sp[:, 3], sp[:, 1], ALU.mult))
            link(dve.tensor_tensor(sp[:, 4], sp[:, 3], sp[:, 3], ALU.mult))
            link(dve.tensor_scalar(sp[:, 5], sp[:, 4], 1 / 17, 1 / 15, ALU.mult, ALU.add))
            for k in (13, 11, 9, 7, 5, 3, 1):
                link(dve.tensor_tensor(sp[:, 5], sp[:, 5], sp[:, 4], ALU.mult))
                link(dve.tensor_scalar(sp[:, 5], sp[:, 5], 1 / k, None, ALU.add))
            link(dve.tensor_tensor(sp[:, 5], sp[:, 5], sp[:, 3], ALU.mult))
            link(dve.tensor_scalar(sp[:, 2], a_real[:], 0.0, 0.5, ALU.max, ALU.mult))
            link(dve.tensor_tensor(sp[:, 5], sp[:, 5], sp[:, 2], ALU.add))
            link(dve.tensor_scalar(mag_k[:], sp[:, 5], LOG_A_SCALE, None, ALU.mult))
            dve.tensor_scalar(mag2_k[:], sp[:, 5], 2 * LOG_A_SCALE, None, ALU.mult).then_inc(dve_consts, 1)
            x_statistics(1)

            def turn_sums(t):
                for c in range(KC):
                    dve.wait_ge(inc_done, KC * t + c + 1)
                    dve.tensor_tensor_scan(turns[:, c], ones[:], turns[:, c], 0.0,
                                           ALU.mult, ALU.add).then_inc(turns_done, 1)

            def rounds(t):
                for c in range(KC):
                    dve.wait_ge(turns_done, KC * t + c + 1)
                    dve.tensor_scalar(frac[:, c], turns[:, c], MAGIC, None, ALU.add).then_inc(round_done, 1)

            def fractions(t):
                for c in range(KC):
                    dve.wait_ge(round_done, KC * t + c + 1)
                    dve.scalar_tensor_tensor(frac[:, c], frac[:, c], MAGIC, turns[:, c],
                                             ALU.subtract, ALU.subtract).then_inc(frac_done, 1)

            def norms(t):
                for c in range(KC):
                    dve.wait_ge(mag2_done, KC * t + c + 1)
                    dve.tensor_scalar(gain[:, c], gain[:, c], 1.0, -1e-6, ALU.subtract,
                                      ALU.min).then_inc(z_done, 1)

            def gains(t):
                for c in range(KC):
                    dve.wait_ge(norm_done, KC * t + c + 1)
                    dve.scalar_tensor_tensor(gain[:, c], tanh_x[:, c], 1.0, gain[:, c],
                                             ALU.add, ALU.mult).then_inc(gain_done, 1)
                for c in range(KC):
                    dve.wait_ge(gain_done, KC * t + c + 1)
                    dve.wait_ge(sin_done, KC * t + c + 1)
                    dve.tensor_tensor(turns[:, c], gain[:, c], sin[:, c], ALU.mult).then_inc(gsin_done, 1)

            def both(plane, c):
                return plane[:, c:c + 1, :].to_broadcast([P, 2, T])

            def rotate_products(t):
                for n, c in enumerate(DVE_CHUNKS):
                    dve.wait_ge(gsin_done, KC * (t + 1))
                    wait(dve, h_done, 2 * KC * t)
                    dve.tensor_tensor(cross[:, :, c], xh[:, :, c], both(turns, c), ALU.mult).then_inc(cross_done, 1)
                for c in range(KC):
                    dve.wait_ge(cos_done, KC * t + c + 1)
                    dve.tensor_tensor(frac[:, c], gain[:, c], cos[:, c], ALU.mult).then_inc(gcos_done, 1)
                for n, c in enumerate(SERVED):
                    if c in DVE_CHUNKS:
                        dve.wait_ge(cross_done, len(DVE_CHUNKS) * t + n + 1)
                    else:
                        dve.wait_ge(cross_pool_done, len(POOL_CHUNKS) * t + n - len(DVE_CHUNKS) + 1)
                    dve.wait_ge(gcos_done, KC * t + c + 1)
                    dve.tensor_tensor(xh[:, :, c], xh[:, :, c], both(frac, c), ALU.mult).then_inc(fwd_mul_done, 1)

                for c in SERVED:
                    dve.wait_ge(fwd_mul_done, KC * t + SERVED.index(c) + 1)
                    dve.tensor_tensor(cross[:, 1, c], xh[:, 0, c], cross[:, 1, c], ALU.add).then_inc(fwd_done, 1)
                    dve.tensor_tensor(cross[:, 0, c], xh[:, 1, c], cross[:, 0, c],
                                      ALU.subtract).then_inc(fwd_done, 1)

            def recur(t):
                wait(dve, out_done, G * t)
                if first(t):
                    dve.wait_ge(win_lo_done, KC)
                dve.wait_ge(carry_done, t + 1)
                dve.wait_ge(mag_done, KC * (t + 1))
                for c in range(KC):
                    for ri in range(2):
                        dve.wait_ge(fwd_done, 2 * (KC * t + SERVED.index(c)) + ri + 1)
                        dve.tensor_tensor_scan(h[:, ri, c], mag[:, c], cross[:, 1 - ri, c], carry[:, ri, c:c + 1],
                                               ALU.mult, ALU.add).then_inc(scan_done, 1)
                for n, c in enumerate(DVE_CHUNKS):
                    dve.wait_ge(scan_done, 2 * (KC * t + c + 1))
                    dve.tensor_tensor(cross[:, :, c], h[:, :, c], both(sin, c), ALU.mult).then_inc(back_cross_done, 1)
                for n, c in enumerate(SERVED):
                    if c in DVE_CHUNKS:
                        dve.wait_ge(back_cross_done, len(DVE_CHUNKS) * t + n + 1)
                    else:
                        dve.wait_ge(back_pool_done, len(POOL_CHUNKS) * t + n - len(DVE_CHUNKS) + 1)
                    dve.tensor_tensor(h[:, :, c], h[:, :, c], both(cos, c), ALU.mult).then_inc(back_mul_done, 1)
                for n, c in enumerate(SERVED):
                    dve.wait_ge(back_mul_done, KC * t + n + 1)
                    dve.tensor_tensor(h[:, 0, c], h[:, 0, c], cross[:, 1, c], ALU.subtract).then_inc(h_done, 1)
                    dve.tensor_tensor(h[:, 1, c], h[:, 1, c], cross[:, 0, c], ALU.add).then_inc(h_done, 1)
                dve.wait_ge(h_done, 2 * KC * (t + 1))
                at = slice(t + 1, t + 2) if isinstance(t, int) else bass.ds(t + 1, 1)
                dve.tensor_scalar(carry[:], h[:, :, :, T - 1], keep[:, at], None, ALU.mult).then_inc(carry_done, 1)

            def y_stat(t, j):
                dve.wait_ge(out_done, G * t + j + 1)
                dve.bn_stats(y_bn[:, j], out_bank(t, j)).then_inc(y_bn_done, 1)

            def y_stat_sum(t, j):
                dve.wait_ge(y_bn_done, G * t + j + 1)
                after_wait(dve)
                dve.bn_aggr(y_mv[:, j], y_bn[:, j]).then_inc(y_stats, 1)

            def y_add(t, j):
                dve.wait_ge(y_normed, G * t + j + 1)
                dve.wait_ge(xres_loaded, 16 * (t + 1))
                dve.tensor_tensor(x_res[:, j], psum[:, OUT0 + j, :], x_res[:, j], ALU.add).then_inc(x1_ready, 1)

            def y_statistics(t):
                for j in range(G):
                    y_stat(t, j)
                    if j > 0:
                        y_stat_sum(t, j - 1)
                y_stat_sum(t, G - 1)

            def step(t):
                if not last(t):
                    xt_low(t + 1, (0, 1, 2))
                turn_sums(t)
                rounds(t)
                norms(t)
                fractions(t)
                if not last(t):
                    xt_low(t + 1, (3,))
                gains(t)
                rotate_products(t)
                if last(t):
                    recur(t)
                if not first(t):
                    y_statistics(t - 1)
                if not (isinstance(t, int) and t >= NT - 2):
                    x_statistics(t + 2)
                if not first(t):
                    for j in range(G):
                        y_add(t - 1, j)
                if not last(t):
                    recur(t)

            step(0)
            with dve.Fori(0, (NT - 2) // 2 - 1) as i:
                for u in range(2):
                    step(2 * i + (1 + u))
            step(NT - 3)
            step(NT - 2)
            step(LAST)
            dve.wait_ge(shared.x1_loaded[0], 16)
            dve.wait_ge(x_stats, G * NT)
            dve.wait_ge(xn_done, G * NT)
            for j in range(G):
                dve.bn_stats(x_bn[:, j], x_in[:, j]).then_inc(shared.x_bn_done, 1)
            for j in range(G):
                dve.wait_ge(shared.x_bn_done, j + 1)
                dve.bn_aggr(x_mv[:, j], x_bn[:, j]).then_inc(shared.x_stats, 1)
            w1_hi, w1_lo = ffn_w1(shared)
            dve.wait_ge(win_done, HC * NT)
            for k in range(KC):
                dve.wait_ge(shared.piece_hi_done, k + 1)
                dve.tensor_tensor(w1_lo[:, 0, k], shared.stage[:, k], w1_hi[:, 0, k].bitcast(F32),
                                  ALU.subtract).then_inc(shared.piece_lo_done, 1)
            for j in range(2):
                y_stat(LAST, j)
                y_stat_sum(LAST, j)
            for j in range(G):
                dve.wait_ge(shared.xt_hi_done, j + 1)
                at = slice(j * P, (j + 1) * P)
                dve.tensor_tensor(xt_lo[:, :, at], psum[:, FFN_BANKS[j], :].rearrange("p (c q) -> p c q", c=KC),
                                  xt_hi[:, :, at].bitcast(F32), ALU.subtract).then_inc(shared.xt_lo_done, 1)
            for j in range(2, G):
                y_stat(LAST, j)
                y_stat_sum(LAST, j)
            dve.wait_ge(xres_loaded, 16 * NT)


def phase_b(nc, d, shared, NQ=NE):
    with ExitStack() as ctx:
        def sb(name, shape, dt=F32):
            return ctx.enter_context(nc.sbuf_tensor(name, shape, dt))

        def sem(name):
            return ctx.enter_context(nc.semaphore(name))

        sw1_hi, sw1_lo = sb("sw1_hi", [P, KC, HS], F32R), sb("sw1_lo", [P, KC, HS], F32R)
        sw3_hi, sw3_lo = sb("sw3_hi", [P, KC, HS], F32R), sb("sw3_lo", [P, KC, HS], F32R)
        sw2_hi, sw2_lo = sb("sw2_hi", [P, HS // P, D], F32R), sb("sw2_lo", [P, HS // P, D], F32R)
        w1_hi, w1_lo = ffn_w1(shared)
        w2_hi, w2_lo = sb("w2_hi", [P, 2, KC, D], F32R), sb("w2_lo", [P, 2, KC, D], F32R)
        stage, xt_hi, xt_lo, x1, xn = shared.stage, shared.xt_hi, shared.xt_lo, shared.rows, shared.xn
        gate = xn[:, 2]
        hid_hi, hid_lo = sb("hid_hi", [P, 2, T], F32R), sb("hid_lo", [P, 2, T], F32R)
        brow_raw = ffn_bias_rows(shared)
        brow_hi = sb("brow_hi", [6, D], F32R)
        brow = sb("brow", [6, D], F32R)
        bsel_raw, low_rows = shared.bsel_raw, shared.low_rows
        bsel = sb("bsel", [6, P], F32R)
        ident = shared.ident
        b_s1, b_s3, b_r1 = shared.b_s1, shared.b_s3, shared.b_r1
        neg_half, x_bn, x_mv, x_sc = shared.neg_half, shared.x_bn, shared.x_mv, shared.x_sc
        y_bn, y_mv, y_sc = shared.y_bn, shared.y_mv, shared.y_sc
        psum = shared.psum
        HID0, OUT0 = 2, 4

        consts_loaded = shared.consts_loaded
        x1_loaded = shared.x1_loaded
        x2_stored = [sem(f"f_x2_stored{k}") for k in range(2)]
        piece_loaded = shared.piece_loaded
        brow_loaded = shared.brow_loaded
        bsel_done = sem("f_bsel_done")
        brow_hi_done = sem("f_brow_hi_done")
        brow_done = sem("f_brow_done")
        piece_hi_done = shared.piece_hi_done
        piece_lo_done = shared.piece_lo_done
        x_bn_done = shared.x_bn_done
        x_stats = shared.x_stats
        x_small = shared.x_small
        xn_done = shared.xn_done
        transposed = shared.transposed
        xt_hi_done = shared.xt_hi_done
        xt_lo_done = shared.xt_lo_done
        hid_mm_done = sem("f_hid_mm_done")
        act_done = sem("f_act_done")
        prod_done = sem("f_prod_done")
        hid_hi_done = sem("f_hid_hi_done")
        hid_lo_done = sem("f_hid_lo_done")
        out_unit_done = sem("f_out_unit_done")
        out_done = sem("f_out_done")
        y_bn_done = sem("f_y_bn_done")
        y_stats = sem("f_y_stats")
        y_small = sem("f_y_small")
        y_scaled = sem("f_y_scaled")
        y_normed = sem("f_y_normed")
        x2_ready = sem("f_x2_ready")

        OLD, SHARED, NEW = range(3)
        kinds = [OLD] * KC + [SHARED] * (HS // P) + [NEW] * KC
        UN = len(kinds)
        starts = [sum(2 if x == SHARED else 1 for x in kinds[:k]) for k in range(UN + 1)]
        HM = starts[UN]

        def steps(eng, step):
            for hf in range(2):
                step(hf, 0, hf, 0)
            if NQ > 2:
                with eng.Fori(0, (NQ - 2) // 2) as i:
                    for v in range(2):
                        for hf in range(2):
                            q = 2 * i + (1 + v)
                            step(4 * i + (2 * (1 + v) + hf), q, hf, (1 + v) % 2)
            for hf in range(2):
                step(2 * (NQ - 1) + hf, NQ - 1, hf, (NQ - 1) % 2)

        def is_last(m):
            return isinstance(m, int) and m == 2 * NQ - 1

        def first(m):
            return isinstance(m, int) and m == 0

        def expert_pieces(slot):
            return ([(w1_hi[:, slot, k], w1_lo[:, slot, k], 1.0) for k in range(KC)]
                    + [(w2_hi[:, slot, k], w2_lo[:, slot, k], 0.5) for k in range(KC)])

        def shared_pieces(half):
            at = slice(half * 512, (half + 1) * 512)
            return ([(sw1_hi[:, k, at], sw1_lo[:, k, at], 1.0) for k in range(KC)]
                    + [(sw3_hi[:, k, at], sw3_lo[:, k, at], 1.0) for k in range(KC)]
                    + [(sw2_hi[:, k], sw2_lo[:, k], 1.0) for k in range(half * KC, half * KC + KC)])

        FIRST = expert_pieces(0) + shared_pieces(0) + shared_pieces(1) + expert_pieces(1)
        NF = len(FIRST)

        def pieces_after(m, q, hf, par, k):
            if first(m):
                cuts = [KC, 8, 12, 16, 20, 23, 26, 29, 32, 34, 36, 38, 40, 40, 40, 40, 40, 40]
                return [(n, FIRST[n]) for n in range(cuts[k + 1], cuts[k + 2])]
            more = not (isinstance(q, int) and q == NQ - 1)
            if hf == 1 and more and 5 <= k < 5 + 8:
                return [(8 * q + (NF + k - 5), expert_pieces(par)[k - 5])]
            return []

        block = ctx.enter_context(nc.Block())

        @block.sync
        def _(sp):
            def load_piece(n, slot, src):
                sp.dma_start(stage[:, slot], src).then_inc(piece_loaded[slot], 16)

            w1d = d["w1"].rearrange("e (k p) n -> e k p n", p=P)
            w2d = d["w2"].rearrange("e (k p) n -> e k p n", p=P)

            def of_expert(j, k):
                src, kk = (w1d, k) if k < KC else (w2d, k - KC)
                if isinstance(j, int):
                    return src[(NE - 1) * j % NE, kk]
                return src[bass.ds((NE - 1) * j % NE, 1), kk].rearrange("e p n -> p (e n)")

            def of_shared(half, k):
                if k < 2 * KC:
                    w = d["sw1"] if k < KC else d["sw3"]
                    return w.rearrange("(k p) n -> k p n", p=P)[k % KC, :, half * 512:(half + 1) * 512]
                return d["sw2"].rearrange("(k p) n -> k p n", p=P)[half * KC + k - 2 * KC]

            sources = ([of_expert(0, k) for k in range(8)] + [of_shared(0, k) for k in range(12)]
                       + [of_shared(1, k) for k in range(12)] + [of_expert(1, k) for k in range(8)])
            for n in range(2 * KC, NF):
                wait(sp, piece_lo_done, n - RING + 1)
                load_piece(n, n % RING, sources[n])
                if n == 3 * KC - 1:
                    sp.wait_ge(shared.x1_ready, G * NT)
                    sp.dma_start(d["x1"].rearrange("(t g p) d -> t p g d", g=G, p=P)[NT - 1], x1[:, 1]).then_inc(
                        shared.x1_stored, 16)
                if n == 5 * KC - 1:
                    sp.wait_ge(shared.x1_stored, 16 * NT)
                    sp.dma_start(x1[:, 1], ffn_rows(d["x1"], 0, 1)).then_inc(x1_loaded[1], 16)

            def step(m, q, hf, par):
                if not first(m):
                    sp.wait_ge(x2_ready, G * m)
                    after_wait(sp)
                    prev_q, prev_hf = (q, 0) if hf == 1 else (q - 1, 1)
                    sp.dma_start(ffn_rows(d["out"], prev_q, prev_hf), x1[:, 1 - hf]).then_inc(x2_stored[1 - hf], 16)
                    if not is_last(m):
                        n_stored = q + 1 if hf == 1 else q
                        sp.wait_ge(x2_stored[1 - hf], 16 * n_stored)
                        after_wait(sp)
                        next_q, next_hf = (q + 1, 0) if hf == 1 else (q, 1)
                        sp.dma_start(x1[:, next_hf], ffn_rows(d["x1"], next_q, next_hf)).then_inc(
                            x1_loaded[next_hf], 16)
                if hf == 0 and not (isinstance(q, int) and q == NQ - 1):
                    sp.wait_ge(brow_done, q + 1)
                    after_wait(sp)
                    rows = d["b_r2"][q + 1:q + 3] if isinstance(q, int) else d["b_r2"][bass.ds(q + 1, 2)]
                    for at in (0, 3):
                        sp.dma_start(brow_raw[at + 1:at + 3, :], rows).then_inc(brow_loaded, 16)
                if hf == 1 and not (isinstance(q, int) and q == NQ - 1):
                    for k in range(8):
                        sp.wait_ge(piece_lo_done, 8 * q + (NF + k - RING + 1))
                        after_wait(sp)
                        load_piece(None, k % RING, of_expert(q + 2, k))

            steps(sp, step)
            sp.wait_ge(x2_ready, G * 2 * NQ)
            sp.dma_start(ffn_rows(d["out"], NQ - 1, 1), x1[:, 1]).then_inc(x2_stored[1], 16)
            for k in range(2):
                sp.wait_ge(x2_stored[k], 16 * NQ)

        @block.gpsimd
        def _(pool):
            def scales(mv, sc, small, n, done, eps):
                after_wait(pool)
                pool.tensor_scalar(sc[:, 0], mv[:, :, 1], eps, 1.0, ALU.add, ALU.mult).then_inc(small, 1)
                pool.tensor_scalar(sc[:, 1], mv[:, :, 0], -1.0, 0.0, ALU.mult, ALU.add).then_inc(small, 1)
                pool.wait_ge(small, n + 2)
                w = sc.shape[-1]
                pool.tensor_tensor(sc[:, 0], sc[:, 0], neg_half[:, 0:w], ALU.pow).then_inc(small, 1)
                pool.wait_ge(small, n + 3)
                pool.tensor_tensor(sc[:, 1], sc[:, 1], sc[:, 0], ALU.mult).then_inc(done, 1)

            def norm_x(m, hf):
                pool.wait_ge(x_stats, G * (m + 1))
                wait(pool, xn_done, G * m)
                scales(x_mv[:], x_sc[:], x_small, 4 * m, x_small, EPS)
                pool.wait_ge(x_small, 4 * m + 4)
                for j in range(G):
                    wait(pool, transposed, G * m + j - 1)
                    after_wait(pool)
                    pool.tensor_scalar(xn[:, j % 2], x1[:, hf, j], x_sc[:, 0, j:j + 1], x_sc[:, 1, j:j + 1],
                                       ALU.mult, ALU.add).then_inc(xn_done, 1)

            def norm_y(m):
                for j in range(G):
                    pool.wait_ge(y_stats, G * m + j + 1)
                    scales(y_mv[:, j:j + 1], y_sc[:, :, j:j + 1], y_small, 3 * (G * m + j), y_scaled, 4 * EPS)

            pool.wait_ge(shared.y_stats, G * NT)
            scales(y_mv[:], y_sc[:], shared.y_small, 3 * (NT - 1), shared.y_scaled, EPS)
            pool.wait_ge(shared.y_normed, G * NT)

            def step(m, q, hf, par):
                if not first(m):
                    norm_y(m - 1)
                if not is_last(m):
                    norm_x(m + 1, 1 - hf)

            steps(pool, step)
            norm_y(2 * NQ - 1)

        @block.tensor
        def _(pe):
            def transposes(m, js):
                for j in js:
                    pe.wait_ge(xn_done, G * m + j + 1)
                    wait(pe, xt_lo_done, G * m + j - 1)
                    for c in range(KC):
                        mm = pe.transpose(psum[:, j % 2, c * P:(c + 1) * P], xn[:, j % 2, c * P:(c + 1) * P],
                                          ident[:])
                    mm.then_inc(transposed, 1)

            def split_product(bank, w_hi, w_lo, at):
                for kc in range(KC):
                    pe.matmul(bank, w_hi[:, kc, at], xt_hi[:, kc], start=(kc == 0), stop=False)
                    pe.matmul(bank, w_hi[:, kc, at], xt_lo[:, kc], start=False, stop=False)
                    mm = pe.matmul(bank, w_lo[:, kc, at], xt_hi[:, kc], start=False, stop=(kc == KC - 1))
                mm.then_inc(hid_mm_done, 1)

            def hidden(m, par, k):
                kind = kinds[k]
                if kind == SHARED:
                    at = slice((k - KC) * P, (k - KC + 1) * P)
                    if k == KC:
                        pe.wait_ge(hid_lo_done, UN * m + k - 1)
                    else:
                        pe.wait_ge(act_done, UN * m + k)
                    split_product(psum[:, HID0, :], sw1_hi, sw1_lo, at)
                    pe.wait_ge(hid_lo_done, UN * m + k)
                    split_product(psum[:, HID0 + 1, :], sw3_hi, sw3_lo, at)
                    return
                c = k if kind == OLD else k - (UN - KC)
                slot = par if kind == OLD else 1 - par
                if kind == NEW and c == 0:
                    pe.wait_ge(act_done, UN * m + k)
                elif kind == NEW and c == 1:
                    pe.wait_ge(hid_lo_done, UN * m + k - 1)
                else:
                    wait(pe, hid_lo_done, UN * m + k - 1)
                split_product(psum[:, HID0 + c % 2, :], w1_hi[:, slot], w1_lo[:, slot],
                              slice(c * P, (c + 1) * P))

            def output(m, q, par, k, js=range(G)):
                kind = kinds[k]
                if kind == SHARED:
                    w_hi, w_lo = sw2_hi[:, k - KC], sw2_lo[:, k - KC]
                else:
                    c = k if kind == OLD else k - (UN - KC)
                    slot = par if kind == OLD else 1 - par
                    w_hi, w_lo = w2_hi[:, slot, c], w2_lo[:, slot, c]
                pe.wait_ge(hid_lo_done, UN * m + k + 1)
                for j in js:
                    at = slice(j * P, (j + 1) * P)
                    bank = psum[:, OUT0 + j, :]
                    if k == 0:
                        wait(pe, x2_ready, G * (m - 1) + j + 1)
                        if j == 0:
                            pe.wait_ge(brow_done, q + 1)
                        if j == 2 and first(m):
                            pe.wait_ge(shared.x1_ready, G * NT)
                        pe.matmul(bank, bsel[:], brow[:], start=True, stop=False)
                    pe.matmul(bank, hid_hi[:, k % 2, at], w_hi, start=False, stop=False)
                    pe.matmul(bank, hid_hi[:, k % 2, at], w_lo, start=False, stop=False)
                    mm = pe.matmul(bank, hid_lo[:, k % 2, at], w_hi, start=False, stop=(k == UN - 1))
                    if k == UN - 1:
                        mm.then_inc(out_done, 1)
                    elif j == G - 1:
                        mm.then_inc(out_unit_done, 1)

            def step(m, q, hf, par):
                pe.wait_ge(xt_lo_done, G * (m + 1))
                for k in range(UN):
                    if first(m) and k in (0, 4, 8, 12):
                        pe.wait_ge(piece_lo_done, {0: KC, 4: 20, 8: 32, 12: 40}[k])
                    elif k == UN - KC and hf == 0 and not first(m):
                        pe.wait_ge(piece_lo_done, 8 * q + NF)
                    if k == UN - 1 and not is_last(m):
                        transposes(m + 1, (0, 1))
                    hidden(m, par, k)
                    if first(m) and k == 1:
                        pe.wait_ge(piece_lo_done, 2 * KC)
                        pe.wait_ge(bsel_done, 1)
                    if k > 0:
                        output(m, q, par, k - 1)
                output(m, q, par, UN - 1, (0, 1))
                if not is_last(m):
                    transposes(m + 1, (2,))
                output(m, q, par, UN - 1, (2,))
                if not is_last(m):
                    transposes(m + 1, (3,))
                output(m, q, par, UN - 1, (3,))

            steps(pe, step)

        @block.scalar
        def _(act):
            def xt_high(m, js):
                for j in js:
                    act.wait_ge(transposed, G * m + j + 1)
                    if j == 0:
                        wait(act, hid_mm_done, HM * m)
                    act.activation(xt_hi[:, :, j * P:(j + 1) * P],
                                   psum[:, j % 2, :].rearrange("p (c q) -> p c q", c=KC),
                                   ACT.Copy).then_inc(xt_hi_done, 1)

            def pieces_high(m, q, hf, par, k):
                for n, (w_hi, _, scale) in pieces_after(m, q, hf, par, k):
                    slot = n % RING if isinstance(n, int) else (k - 5) % RING
                    turn = n // RING if isinstance(n, int) else 2 * q + (NF + k - 5) // RING
                    act.wait_ge(piece_loaded[slot], 16 * (turn + 1))
                    if not first(m):
                        act.wait_ge(out_unit_done, (UN - 1) * m + KC)
                    act.activation(w_hi, stage[:, slot], ACT.Copy, scale=scale).then_inc(piece_hi_done, 1)

            def activate(m, q, k):
                kind = kinds[k]
                act.wait_ge(hid_mm_done, HM * m + starts[k] + 1)
                if kind == SHARED:
                    wait(act, prod_done, (HS // P) * m + k - KC)
                    act.activation(gate, psum[:, HID0, :], ACT.Silu,
                                   bias=b_s1[:, k - KC:k - KC + 1]).then_inc(act_done, 1)
                else:
                    c = k if kind == OLD else k - (UN - KC)
                    j = q if kind == OLD else q + 1
                    col = KC * j + c
                    at = slice(col, col + 1) if isinstance(col, int) else bass.ds(col, 1)
                    bank = psum[:, HID0 + c % 2, :]
                    after_wait(act)
                    act.activation(bank, bank, ACT.Gelu, bias=b_r1[:, at]).then_inc(act_done, 1)

            def hidden_high(m, k):
                kind = kinds[k]
                if kind == SHARED:
                    act.wait_ge(prod_done, (HS // P) * m + k - KC + 1)
                    bank = psum[:, HID0 + 1, :]
                else:
                    act.wait_ge(act_done, UN * m + k + 1)
                    bank = psum[:, HID0 + (k if kind == OLD else k - (UN - KC)) % 2, :]
                if k >= 2:
                    act.wait_ge(out_unit_done, (UN - 1) * m + k - 1)
                elif k == 1:
                    wait(act, out_done, G * m)
                else:
                    wait(act, out_unit_done, (UN - 1) * m)
                act.activation(hid_hi[:, k % 2], bank, ACT.Copy).then_inc(hid_hi_done, 1)

            def bias_rows_high(q):
                act.wait_ge(brow_loaded, 32 * (q + 1))
                act.activation(brow_hi[:], brow_raw, ACT.Copy).then_inc(brow_hi_done, 1)

            def y_normalise(m, js):
                for j in js:
                    act.wait_ge(y_scaled, G * m + j + 1)
                    bank = psum[:, OUT0 + j, :]
                    act.activation(bank, bank, ACT.Identity, bias=y_sc[:, 1, j:j + 1],
                                   scale=y_sc[:, 0, j:j + 1]).then_inc(y_normed, 1)

            act.wait_ge(consts_loaded, 16 * 7)
            act.activation(bsel[:], bsel_raw[:], ACT.Copy).then_inc(bsel_done, 1)
            bias_rows_high(0)
            pieces_high(0, 0, 0, 0, -1)
            act.wait_ge(shared.y_scaled, NT)
            for j, bank in enumerate(shared.last_out_banks):
                act.activation(psum[:, bank], psum[:, bank], ACT.Identity, bias=y_sc[:, 1, j:j + 1],
                               scale=y_sc[:, 0, j:j + 1]).then_inc(shared.y_normed, 1)

            def step(m, q, hf, par):
                if not first(m):
                    y_normalise(m - 1, (0,))
                for k in range(UN):
                    activate(m, q, k)
                    hidden_high(m, k)
                    if k == 0 and not first(m):
                        y_normalise(m - 1, (1, 2, 3))
                    pieces_high(m, q, hf, par, k)
                    if k == 4 and hf == 1 and not is_last(m):
                        bias_rows_high(q + 1)
                if not is_last(m):
                    xt_high(m + 1, range(G))

            steps(act, step)
            y_normalise(2 * NQ - 1, range(G))

        @block.vector
        def _(dve):
            def x_statistics(m, q, hf):
                dve.wait_ge(x1_loaded[hf], 16 * (q + 1))
                wait(dve, x_stats, G * m)
                wait(dve, xn_done, G * m)
                for j in range(G):
                    dve.bn_stats(x_bn[:, j], x1[:, hf, j]).then_inc(x_bn_done, 1)
                for j in range(G):
                    dve.wait_ge(x_bn_done, G * m + j + 1)
                    after_wait(dve)
                    dve.bn_aggr(x_mv[:, j], x_bn[:, j]).then_inc(x_stats, 1)

            def xt_low(m, js):
                for j in js:
                    dve.wait_ge(xt_hi_done, G * m + j + 1)
                    at = slice(j * P, (j + 1) * P)
                    dve.tensor_tensor(xt_lo[:, :, at], psum[:, j % 2, :].rearrange("p (c q) -> p c q", c=KC),
                                      xt_hi[:, :, at].bitcast(F32), ALU.subtract).then_inc(xt_lo_done, 1)

            def pieces_low(m, q, hf, par, k):
                for n, (w_hi, w_lo, scale) in pieces_after(m, q, hf, par, k):
                    slot = n % RING if isinstance(n, int) else (k - 5) % RING
                    dve.wait_ge(piece_hi_done, n + 1)
                    dve.scalar_tensor_tensor(w_lo, stage[:, slot], scale, w_hi.bitcast(F32), ALU.mult,
                                             ALU.subtract).then_inc(piece_lo_done, 1)

            def product(m, k):
                if kinds[k] != SHARED:
                    return
                bank = psum[:, HID0 + 1, :]
                dve.wait_ge(hid_mm_done, HM * m + starts[k] + 2)
                dve.wait_ge(act_done, UN * m + k + 1)
                dve.scalar_tensor_tensor(bank, bank, b_s3[:, k - KC:k - KC + 1], gate, ALU.add,
                                         ALU.mult).then_inc(prod_done, 1)

            def hidden_low(m, k):
                kind = kinds[k]
                bank = psum[:, HID0 + (1 if kind == SHARED else (k if kind == OLD else k - (UN - KC)) % 2), :]
                dve.wait_ge(hid_hi_done, UN * m + k + 1)
                dve.tensor_tensor(hid_lo[:, k % 2], bank, hid_hi[:, k % 2].bitcast(F32),
                                  ALU.subtract).then_inc(hid_lo_done, 1)

            def bias_rows(q):
                dve.wait_ge(brow_hi_done, q + 1)
                if not (isinstance(q, int) and q == 0):
                    dve.wait_ge(out_unit_done, 2 * (UN - 1) * q - (UN - 1) + 1)
                dve.scalar_tensor_tensor(brow[:], brow_hi[:].bitcast(F32), low_rows[:, 0:1], brow_raw,
                                         ALU.mult, ALU.add).then_inc(brow_done, 1)

            def y_stat(m, j):
                bank = psum[:, OUT0 + j, :]
                dve.wait_ge(out_done, G * m + j + 1)
                dve.bn_stats(y_bn[:, j], bank).then_inc(y_bn_done, 1)
                dve.wait_ge(y_bn_done, G * m + j + 1)
                after_wait(dve)
                dve.bn_aggr(y_mv[:, j], y_bn[:, j]).then_inc(y_stats, 1)

            def y_add(m, hf, j):
                dve.wait_ge(y_normed, G * m + j + 1)
                dve.tensor_tensor(x1[:, hf, j], psum[:, OUT0 + j, :], x1[:, hf, j], ALU.add).then_inc(x2_ready, 1)

            dve.wait_ge(consts_loaded, 16 * 7)
            bias_rows(0)
            pieces_low(0, 0, 0, 0, -1)
            for j, bank in enumerate(shared.last_out_banks):
                dve.wait_ge(shared.y_normed, G * (NT - 1) + j + 1)
                dve.tensor_tensor(x1[:, 1, j], psum[:, bank], x1[:, 1, j], ALU.add).then_inc(shared.x1_ready, 1)

            def step(m, q, hf, par):
                prev = 1 - hf
                if not first(m):
                    for j in range(G):
                        y_stat(m - 1, j)
                    y_add(m - 1, prev, 0)
                for k in range(UN):
                    product(m, k)
                    hidden_low(m, k)
                    if k == 0 and not first(m):
                        for j in range(1, G):
                            y_add(m - 1, prev, j)
                    pieces_low(m, q, hf, par, k)
                    if k == 4 and hf == 1 and not is_last(m):
                        bias_rows(q + 1)
                    if k == 10 and not is_last(m):
                        x_statistics(m + 1, q if hf == 0 else q + 1, 1 - hf)
                if not is_last(m):
                    xt_low(m + 1, range(G))

            steps(dve, step)
            for j in range(G):
                y_stat(2 * NQ - 1, j)
            for j in range(G):
                y_add(2 * NQ - 1, 1, j)



def lay_out(inputs):
    import numpy as np

    def rows(w):
        return np.ascontiguousarray(w.reshape(-1, P, w.shape[-1]).transpose(1, 0, 2))

    def cols(v):
        return np.ascontiguousarray(v.reshape(-1, P).T)

    a = {k.removeprefix("L0_"): np.asarray(v) for k, v in inputs.items()}
    gate_b = np.concatenate([a["attn_b_gx"].reshape(HC, 64), a["attn_b_ga"].reshape(HC, 64)], axis=1).T
    return {
        "x": np.ascontiguousarray(a["attn_x"].reshape(N, D)),
        "w_in": rows(a["attn_w_in"]),
        "b_in": cols(a["attn_b_in"]),
        "w_gate": np.ascontiguousarray(np.concatenate([a["attn_w_gx"], a["attn_w_ga"]], axis=2).transpose(1, 0, 2)),
        "b_gate": np.ascontiguousarray(gate_b),
        "a_real": cols(a["attn_a_real_param"]),
        "a_imag": cols(a["attn_a_imag_param"]),
        "w_out": rows(a["attn_w_out"]),
        "b_out": np.ascontiguousarray(np.stack([a["attn_b_out"]] * 2)),
        "low_row": np.array([[0.0], [-1.0]], np.float32),
        "ident": np.eye(P, dtype=np.float32),
        "sw1": a["ffn_sw1"], "sw3": a["ffn_sw3"], "sw2": a["ffn_sw2"], "w1": a["ffn_w1"], "w2": a["ffn_w2"],
        "b_s1": cols(a["ffn_sb1"]),
        "b_s3": cols(a["ffn_sb3"]),
        "b_s2": np.ascontiguousarray(a["ffn_sb2"].reshape(1, D)),
        "b_r1": cols(np.concatenate([a["ffn_b1"][-j % NE] for j in range(NE + 1)])),
        "b_r2": np.ascontiguousarray(np.stack([a["ffn_b2"][-j % NE] for j in range(NE + 1)])),
        "bsel": np.repeat(np.array([[1.0], [0.5], [0.5]] * 2, np.float32), P, axis=1),
        "low_rows": np.repeat(np.array([[0.0], [-1.0]], np.float32), 3, axis=0),
    }


def sandwich(nc, d):
    d["x1"] = nc.dram_tensor("x1_rows", (N, D), F32).ap()
    with ExitStack() as ctx:
        shared = Shared(nc, ctx)
        phase_a(nc, d, shared)
        phase_b(nc, d, shared)


def kernel(**inputs):
    import concourse.bacc as bacc
    from concourse.bass_utils import run_bass_kernel_spmd

    nc = bacc.Bacc("TRN2", target_bir_lowering=False, num_devices=1, dynamic_dma_scratch_size=1024)
    arrays = {f"in_{k}": v for k, v in lay_out(inputs).items()}
    d = {k[3:]: nc.dram_tensor(k, v.shape, F32, kind="ExternalInput").ap() for k, v in arrays.items()}
    d["out"] = nc.dram_tensor("out_rows", (N, D), F32, kind="ExternalOutput").ap()
    sandwich(nc, d)
    r = run_bass_kernel_spmd(nc, [arrays], core_ids=[0])
    return r.results[0]["out_rows"].reshape(B, S, D)
```
